# Optimizing a Trainium2 kernel written in Bass

```python
import numpy as np
import jax
import jax.numpy as jnp

def _softmax(x, axis=-1):
    return jax.nn.softmax(x, axis=axis)

def _gelu(x):
    return jax.nn.gelu(x, approximate=True)

def _silu(x):
    return jax.nn.silu(x)

def _sigmoid(x):
    return jax.nn.sigmoid(x)

def _layernorm(x, axis=-1, eps=1e-05):
    m = jnp.mean(x, axis=axis, keepdims=True)
    v = jnp.var(x, axis=axis, keepdims=True)
    return (x - m) / jnp.sqrt(v + eps)

def _scatter_add(tgt, idx, src, axis=0):
    return tgt.at[idx].add(src)

def _segment_sum(src, seg, n):
    return jax.ops.segment_sum(src, seg, n)
kernel_name = 'mk_adj_resnorm_d1_adj_r2_c1aaba'

def setup_inputs(seed: int=0):
    np.random.seed(seed)
    _w = jnp.asarray

    def _rec_inputs():
        import jax
        import jax.numpy as jnp
        _gk = jax.random.key(seed)
        x = -0.003407 + 1.001 * jax.random.normal(jax.random.fold_in(_gk, 1), (32, 256, 64), jnp.float32)
        _a = jax.random.bernoulli(jax.random.fold_in(_gk, 2), 0.0625, (32, 256, 256))
        _a = jnp.logical_or(_a, jnp.swapaxes(_a, -1, -2))
        _a = jnp.logical_or(_a, jnp.eye(256, dtype=bool))
        _af = _a.astype(jnp.float32)
        adj = _af
        return (x, adj)
    x, adj = _rec_inputs()

    def _L0_gnn_setup():
        import jax, jax.numpy as jnp
        import numpy as np
        B, N, DIN, DOUT = (8, 128, 64, 64)
        AVG_D_LOG = 4.86
        EPS = 1e-05
        NEG_BIG = 1000000000.0
        N_AGG, N_SCALE = (4, 3)

        def _pna_forward(x, adj, W_pre, b_pre, W_post, b_post):
            n = adj.shape[1]
            h_i = jnp.broadcast_to(x[:, :, None, :], (x.shape[0], n, n, x.shape[-1]))
            h_j = jnp.broadcast_to(x[:, None, :, :], (x.shape[0], n, n, x.shape[-1]))
            h_cat = jnp.concatenate([h_i, h_j], axis=-1)
            h_mod = jnp.einsum('bnme,ed->bnmd', h_cat, W_pre) + b_pre
            deg = adj.sum(-1)
            deg_safe = jnp.maximum(deg, 1.0)[..., None]
            mask = (adj > 0)[..., None]
            s1 = jnp.einsum('bnm,bnmd->bnd', adj, h_mod)
            mean = s1 / deg_safe
            s2 = jnp.einsum('bnm,bnmd->bnd', adj, h_mod * h_mod)
            var = jax.nn.relu(s2 / deg_safe - mean * mean)
            std = jnp.sqrt(var + EPS)
            mx = jnp.max(jnp.where(mask, h_mod, -NEG_BIG), axis=2)
            mn = jnp.min(jnp.where(mask, h_mod, NEG_BIG), axis=2)
            m = jnp.concatenate([mean, mx, mn, std], axis=-1)
            log_deg = jnp.log(deg + 1.0)[..., None]
            amp = m * (log_deg / AVG_D_LOG)
            att = m * (AVG_D_LOG / jnp.maximum(log_deg, EPS))
            m_all = jnp.concatenate([m, amp, att], axis=-1)
            m_cat = jnp.concatenate([x, m_all], axis=-1)
            return jnp.einsum('bne,ed->bnd', m_cat, W_post) + b_post
        key = jax.random.key(seed)
        k1, k2, k3, k4, k5, k6 = jax.random.split(key, 6)
        inp = jax.random.normal(k1, (B, N, DIN), dtype=jnp.float32)
        adj = jax.random.randint(k2, (B, N, N), 0, 2).astype(jnp.float32)
        W_pre = jax.random.normal(k3, (2 * DIN, DIN), dtype=jnp.float32) / np.sqrt(2 * DIN)
        b_pre = jnp.zeros((DIN,), dtype=jnp.float32)
        post_in = (N_AGG * N_SCALE + 1) * DIN
        W_post = jax.random.normal(k4, (post_in, DOUT), dtype=jnp.float32) / np.sqrt(post_in)
        b_post = jnp.zeros((DOUT,), dtype=jnp.float32)
        return {'input': inp, 'adj': adj, 'W_pre': W_pre, 'b_pre': b_pre, 'W_post': W_post, 'b_post': b_post}
    _L0_gnn_all = _L0_gnn_setup()
    _L0_gnn_in = {k: v for k, v in _L0_gnn_all.items() if k in ('W_pre', 'b_pre', 'W_post', 'b_post')}
    del _L0_gnn_all
    return {'x': x, 'adj': adj, 'L0_gnn_W_pre': _L0_gnn_in['W_pre'], 'L0_gnn_b_pre': _L0_gnn_in['b_pre'], 'L0_gnn_W_post': _L0_gnn_in['W_post'], 'L0_gnn_b_post': _L0_gnn_in['b_post']}

def reference(x, adj, L0_gnn_W_pre, L0_gnn_b_pre, L0_gnn_W_post, L0_gnn_b_post):
    import jax
    import jax.numpy as jnp

    def _L0_gnn_ref(input, adj, W_pre, b_pre, W_post, b_post):
        import jax, jax.numpy as jnp
        import numpy as np
        B, N, DIN, DOUT = (8, 128, 64, 64)
        AVG_D_LOG = 4.86
        EPS = 1e-05
        NEG_BIG = 1000000000.0
        N_AGG, N_SCALE = (4, 3)

        def _pna_forward(x, adj, W_pre, b_pre, W_post, b_post):
            n = adj.shape[1]
            h_i = jnp.broadcast_to(x[:, :, None, :], (x.shape[0], n, n, x.shape[-1]))
            h_j = jnp.broadcast_to(x[:, None, :, :], (x.shape[0], n, n, x.shape[-1]))
            h_cat = jnp.concatenate([h_i, h_j], axis=-1)
            h_mod = jnp.einsum('bnme,ed->bnmd', h_cat, W_pre) + b_pre
            deg = adj.sum(-1)
            deg_safe = jnp.maximum(deg, 1.0)[..., None]
            mask = (adj > 0)[..., None]
            s1 = jnp.einsum('bnm,bnmd->bnd', adj, h_mod)
            mean = s1 / deg_safe
            s2 = jnp.einsum('bnm,bnmd->bnd', adj, h_mod * h_mod)
            var = jax.nn.relu(s2 / deg_safe - mean * mean)
            std = jnp.sqrt(var + EPS)
            mx = jnp.max(jnp.where(mask, h_mod, -NEG_BIG), axis=2)
            mn = jnp.min(jnp.where(mask, h_mod, NEG_BIG), axis=2)
            m = jnp.concatenate([mean, mx, mn, std], axis=-1)
            log_deg = jnp.log(deg + 1.0)[..., None]
            amp = m * (log_deg / AVG_D_LOG)
            att = m * (AVG_D_LOG / jnp.maximum(log_deg, EPS))
            m_all = jnp.concatenate([m, amp, att], axis=-1)
            m_cat = jnp.concatenate([x, m_all], axis=-1)
            return jnp.einsum('bne,ed->bnd', m_cat, W_post) + b_post
        return _pna_forward(input, adj, W_pre, b_pre, W_post, b_post)
    x = _layernorm(x + _L0_gnn_ref(x, adj, L0_gnn_W_pre, L0_gnn_b_pre, L0_gnn_W_post, L0_gnn_b_post), axis=-1)
    return x

_drawn_inputs = setup_inputs


def setup_inputs(seed=0):
    import zlib

    import numpy as np

    out = dict(_drawn_inputs(seed))
    spreads = {'L0_gnn_b_pre': (0.0, 0.1), 'L0_gnn_b_post': (0.0, 0.1)}
    factors = {}
    for name, (base, spread) in spreads.items():
        noise = np.random.default_rng([zlib.crc32(name.encode()), seed]).standard_normal(out[name].shape)
        drawn = base * np.exp(spread * noise) if base else spread * noise
        out[name] = jnp.asarray(drawn.astype(out[name].dtype))
    for name, factor in factors.items():
        out[name] = (out[name] * factor).astype(out[name].dtype)
    return out
```

```python
from contextlib import ExitStack

import numpy as np

import concourse.bass as bass
from concourse import mybir

F32 = mybir.dt.float32
BF16 = mybir.dt.bfloat16
ALU = mybir.AluOpType
ACT = mybir.ActivationFunctionType
AX = mybir.AxisListType

P = 128
B, N, D = 32, 256, 64
H = N // P
K = 5
S = 2 ** K
TILES = P // S
GH = -(-P // K)
G = H * GH
R = G // TILES
PAD = GH * K
MAIN = 2 * -(-R // 2)
FILLS = -(-R // 2)
TFILLS = -(-R // 4)
J = 3
AVG_D_LOG = 4.86
EPS = 1e-05
EMPTY = -1e9
CH = 4
CHUNKS = B // CH
STATS = 9
STORE_LAG = 6
DEG_SMALL = 4
LOOP_FIRST, UNROLL = 8, 4
LOOP_TRIPS = (B - LOOP_FIRST) // UNROLL


def constants():
    sign = np.zeros((P, H, R // H + 1, P), np.float32)
    for g in range(G):
        k, r, j = g // GH, g // TILES, g % TILES
        for i in range(K):
            m = K * (g % GH) + i
            if m < P:
                for s in range(S):
                    sign[m, k, r - (R // H) * k, S * j + s] = 1 if s >> i & 1 else -1
    bias = np.array([[1.0 - bin(s % S).count("1")] for s in range(P)], np.float32)
    return np.eye(P, dtype=np.float32), sign.reshape(P, -1), bias


def pna_layer(nc, x, adj, w_pre, b_pre, w_post, b_post, ident_in, sign_fn, bias_in, out):
    with ExitStack() as ctx:
        def sb(name, shape, dt=F32):
            return ctx.enter_context(nc.sbuf_tensor(name, shape, dt))

        def sem(name):
            return ctx.enter_context(nc.semaphore(name))

        ident = sb("ident", [P, P])
        sign_f = sb("sign_f", [P, H, R // H + 1, P])
        sign = sb("sign", [P, H, R // H + 1, P], BF16)
        hot_bias = sb("hot_bias", [P, 1])
        w_pq = sb("w_pq", [D + 1, 2 * D])
        w_qq = sb("w_qq", [D, 2 * D])
        w_pT = sb("w_pT", [D, D + 1])
        w_fold = sb("w_fold", [D, 2, J, D])
        w_sum = sb("w_sum", [D, J, D])
        w_x = sb("w_x", [D + 1, J, D])
        w_x0 = sb("w_x0", [D + 1, D])
        w_ms = sb("w_ms", [P, J, D])
        w_mx = sb("w_mx", [P, J, D])
        w_mean = sb("w_mean", [P, 3, J])
        adj_all = sb("adj_all", [P, 2, CH, H, N])
        deg = sb("deg", [P, B * H])
        deg1 = sb("deg1", [P, B * H])
        deg_safe = sb("deg_safe", [P, B * H])
        deg_inv = sb("deg_inv", [P, B * H])
        deg_part = sb("deg_part", [P, B * H])
        scaler = sb("scaler", [P, B * H, 2])
        x_in = [sb(f"x_in{i}", [P, H, D]) for i in range(2)]
        adj_in = [sb(f"adj_in{i}", [P, H, N]) for i in range(2)]
        adjT = [sb(f"adjT{i}", [P, H, N]) for i in range(2)]
        mask = [sb(f"mask{i}", [P, H, N], BF16) for i in range(2)]
        xT = [sb(f"xT{i}", [D + 1, H, PAD]) for i in range(4)]
        pq = [sb(f"pq{i}", [P, H, 3, D]) for i in range(2)]
        table = [sb(f"table{i}", [P, G, S]) for i in range(2)]
        tableT = [sb(f"tableT{i}", [P, R, P]) for i in range(2)]
        hot = [sb(f"hot{i}", [P, R, N]) for i in range(2)]
        acc = [sb(f"acc{i}", [P, 2, 2, N]) for i in range(2)]
        folded = sb("folded", [P, 2, N])
        best = [sb(f"best{i}", [P, N]) for i in range(2)]
        uv = [sb(f"uv{i}", [P, H, 2, D]) for i in range(2)]
        pool_a = sb("pool_a", [P, H, D])
        pool_b = sb("pool_b", [P, H, D])
        pool_c = sb("pool_c", [P, H, D])
        var = [sb(f"var{i}", [P, H, D]) for i in range(2)]
        ms = [sb(f"ms{i}", [P, H, 2, D]) for i in range(2)]
        msT = [sb(f"msT{i}", [P, H, P]) for i in range(2)]
        z = [sb(f"z{i}", [P, H, J, D]) for i in range(2)]
        zs = sb("zs", [P, H, 2, D])
        y1 = sb("y1", [P, H, D])
        y = [sb(f"y_out{i}", [P, H, D]) for i in range(2)]
        y_sq = sb("y_sq", [P, H, D])
        sumsq = sb("sumsq", [P, 2, H])
        root = sb("root", [P, 2, H])
        rstd = sb("rstd", [P, 2, H])
        result = [sb(f"result{i}", [P, H, D]) for i in range(2)]
        eps_col = sb("eps_col", [P, 1])

        ps_main = [ctx.enter_context(nc.psum_tensor(f"ps_main{i}", [P, 2, 2, N], F32)) for i in range(2)]
        ps_hot = [ctx.enter_context(nc.psum_tensor(f"ps_hot{i}", [P, 2, N], F32)) for i in range(2)]
        ps_a = ctx.enter_context(nc.psum_tensor("ps_a", [P, 4 * P], F32))
        ps_b = ctx.enter_context(nc.psum_tensor("ps_b", [P, 4 * P], F32))

        s_const = sem("const_loaded")
        s_x = [sem(f"x_loaded{i}") for i in range(2)]
        s_adj = [sem(f"adj_loaded{i}") for i in range(2)]
        s_all = [sem(f"adj_chunk_loaded{i}") for i in range(2)]
        s_out = [sem(f"stored{i}") for i in range(2)]
        s_fill = sem("fills_done")
        s_setup = sem("setup_step")
        s_setup_pe = sem("setup_pe")
        s_signs = sem("signs_ready")
        s_deg = sem("deg_step")
        s_log = sem("log_ready")
        s_adjT_ps = sem("adjT_in_psum")
        s_xT_ps = sem("xT_in_psum")
        s_q_ps = sem("q_in_psum")
        s_pq_ps = sem("pq_in_psum")
        s_tabT_ps = sem("tableT_in_psum")
        s_hot_ps = sem("hot_in_psum")
        s_sum_ps = sem("sums_in_psum")
        s_msT_ps = sem("msT_in_psum")
        s_z_ps = sem("z_in_psum")
        s_round = sem("round_in_psum")
        s_adjT = sem("adjT_ready")
        s_xT = sem("xT_ready")
        s_p = sem("p_ready")
        s_pq = sem("pq_ready")
        s_tabT = sem("tableT_ready")
        s_hot = sem("hot_ready")
        s_uv = sem("uv_ready")
        s_std = sem("std_ready")
        s_msT = sem("msT_ready")
        s_acc0 = sem("acc_started")
        s_z = sem("z_copied")
        s_sq = sem("sumsq_ready")
        s_root = sem("root_ready")
        s_tab = sem("table_step")
        s_acc = sem("acc_step")
        s_fold = sem("fold_step")
        s_rstd = sem("rstd_ready")
        s_go_x = sem("go_x_transposes")
        s_go_mask = sem("go_mask")
        s_go_var = sem("go_var")
        s_mask = sem("mask_ready")
        s_stat = sem("stats_step")
        s_y = sem("y_step")
        s_res = sem("result_ready")

        def wait(eng, s, value):
            if not isinstance(value, int) or value > 0:
                eng.wait_ge(s, value)

        def half(b, c):
            return 8 * b + (16 - 8 * (c % 2))

        def at(s, n):
            return isinstance(s, int) and s == n

        def steps(eng, one_step):
            def has(s):
                return "".join(n for i, n in enumerate("PQMZ") if 0 <= s - i < B)
            for s in range(LOOP_FIRST):
                one_step(s, s % 4, has(s))
            with eng.Fori(0, LOOP_TRIPS) as i:
                for u in range(UNROLL):
                    one_step(UNROLL * i + (LOOP_FIRST + u), u, "PQMZ")
            for s in range(B, B + 3):
                one_step(s, s % 4, has(s))

        x_rows = x.rearrange("b (p t) d -> b p t d", t=H)
        adj_rows = adj.rearrange("b (p t) m -> b p t m", t=H)
        out_rows = out.rearrange("b (p t) d -> b p t d", t=H)
        post = w_post[D:, :].rearrange("(j k d) o -> k d j o", j=J, k=4)
        CONST_LOADS = 15
        FILLED = 13
        SET_UP = 21

        DEG_FIRST = 1 + DEG_SMALL
        DEG_ALL = CHUNKS + 2 * DEG_SMALL

        block = ctx.enter_context(nc.Block())

        @block.sync
        def _(sp):
            def load(b, c):
                wait(sp, s_adjT_ps, b - 1)
                sp.dma_start(adj_in[c % 2][:], adj_rows[b]).then_inc(s_adj[c % 2], 16)
                wait(sp, s_xT_ps, b - 1)
                sp.dma_start(x_in[c % 2][:], x_rows[b]).then_inc(s_x[c % 2], 16)

            loads = [
                (ident[:], ident_in), (sign_f[:].rearrange("p a b c -> p (a b c)"), sign_fn), (hot_bias[:], bias_in),
                (w_pq[0:D, 0:D], w_pre[0:D, :]), (w_pq[D:D + 1, 0:D], b_pre.rearrange("(a d) -> a d", a=1)),
                (w_pq[0:D, D:2 * D], w_pre[D:2 * D, :]), (w_qq[:, 0:D], w_pre[D:2 * D, :]),
                (w_x0[0:D, :], w_post[0:D, :]), (w_x0[D:D + 1, :], b_post.rearrange("(a d) -> a d", a=1)),
                (w_ms[0:D, :, :], post[0]), (w_ms[D:2 * D, :, :], post[3]),
                (w_mx[0:D, :, :], post[1]), (w_mx[D:2 * D, :, :], post[2]),
                (w_fold[:, 0, :, :], post[1]), (w_fold[:, 1, :, :], post[2]),
            ]
            assert len(loads) == CONST_LOADS
            sp.dma_start(*loads[0]).then_inc(s_const, 16)
            load(0, 0)
            for dst, src in loads[1:]:
                sp.dma_start(dst, src).then_inc(s_const, 16)
            load(1, 1)
            for c in range(CHUNKS):
                if c >= 2:
                    sp.wait_ge(s_deg, 1 if c == 2 else 1 + DEG_SMALL + c - 2)
                sp.dma_start(adj_all[:, c % 2], adj_rows[CH * c:CH * c + CH].rearrange("b p t m -> p b t m")) \
                    .then_inc(s_all[c % 2], 16)
                if c in (1, 3):
                    load((c + 3) // 2, (c + 3) // 2)

            def store(b, c):
                wait(sp, s_res, b + 1)
                sp.dma_start(out_rows[b], result[c % 2][:]).then_inc(s_out[c % 2], 16)

            for b in range(UNROLL, 2 * UNROLL):
                load(b, b % 4)
                if b >= STORE_LAG:
                    store(b - STORE_LAG, (b - STORE_LAG) % 4)
            with sp.Fori(0, B // UNROLL - 2) as i:
                for u in range(UNROLL):
                    load(UNROLL * i + (2 * UNROLL + u), u)
                    store(UNROLL * i + (2 * UNROLL + u - STORE_LAG), (u - STORE_LAG) % 4)
            for b in range(B - STORE_LAG, B):
                store(b, b % 4)
            for c in range(2):
                sp.wait_ge(s_out[c], 16 * B // 2)

        @block.tensor
        def _(pe):
            wait(pe, s_const, 16 * CONST_LOADS)
            wait(pe, s_fill, FILLED)
            pe.transpose(ps_b[0:D, 0:D + 1], w_pq[:, 0:D], ident[0:D + 1, 0:D + 1]).then_inc(s_setup_pe, 1)
            pe.wait_ge(s_setup, 2)
            pe.matmul(ps_b[0:D + 1, 0:J * D], w_pT[:], w_sum[:].rearrange("d j o -> d (j o)"), start=True, stop=True) \
                .then_inc(s_setup_pe, 1)

            def adj_transposes(b, c):
                wait(pe, s_adj[c % 2], half(b, c))
                wait(pe, s_pq, b)
                wait(pe, s_tabT, TFILLS * (b - 1))
                for k in range(H):
                    for t in range(H):
                        last = pe.transpose(ps_a[:, (k * H + t) * P:(k * H + t + 1) * P],
                                            adj_in[c % 2][:, t, k::H], ident[:])
                last.then_inc(s_adjT_ps, 1)

            def x_transposes(b, c):
                wait(pe, s_x[c % 2], half(b, c))
                wait(pe, s_adjT, b + 1)
                pe.sem_inc(s_go_x, 1)
                for t in range(H):
                    last = pe.transpose(ps_a[0:D, t * P:(t + 1) * P], x_in[c % 2][:, t, :], ident[:])
                last.then_inc(s_xT_ps, 1)

            def q_rows(b, c):
                wait(pe, s_xT, b + 1)
                wait(pe, s_tab, K * b)
                wait(pe, s_msT, b - 1)
                wait(pe, s_z, b - 2)
                pe.matmul(ps_b[:, 0:H * PAD], w_qq[:], xT[c % 4][0:D].rearrange("d t m -> d (t m)"),
                          start=True, stop=True).then_inc(s_q_ps, 1)

            def pq_nodes(b, c):
                wait(pe, s_xT, b + 1)
                wait(pe, s_tabT, TFILLS * (b - 1) + 2)
                for t in range(H):
                    last = pe.matmul(ps_a[:, t * P:(t + 1) * P], xT[c % 4][:, t, 0:P], w_pq[:], start=True, stop=True)
                last.then_inc(s_pq_ps, 1)

            def hot_rows(b, c, f):
                wait(pe, s_hot, FILLS * b + f - 1)
                for r in range(2 * f, min(2 * f + 2, R)):
                    ks = [k for k in range(H) if (R // H) * k <= r <= (R // H) * (k + 1)]
                    for k in ks:
                        last = pe.matmul(ps_hot[(c + f) % 2][:, r % 2, :], sign[:, k, r - (R // H) * k, :],
                                         mask[c % 2][:, k, :], start=(k == ks[0]), stop=(k == ks[-1]))
                last.then_inc(s_hot_ps, 1)

            def table_transposes(b, c, f, has):
                if f == 0 and "P" in has:
                    wait(pe, s_xT, b + 2)
                if f == 2 and "P" in has:
                    wait(pe, s_pq, b + 2)
                wait(pe, s_tabT, TFILLS * b + f)
                for r in range(4 * f, min(4 * f + 4, R)):
                    last = pe.transpose(ps_a[:, (r % 4) * P:(r % 4 + 1) * P],
                                        table[c % 2][:, TILES * r:TILES * r + TILES, :].rearrange("p g s -> p (g s)"),
                                        ident[:])
                last.then_inc(s_tabT_ps, 1)

            def neighbour_sums(b, c, has):
                wait(pe, s_adjT, b + 1)
                wait(pe, s_pq, b + 1)
                if "P" in has:
                    wait(pe, s_tab, K * (b + 2))
                wait(pe, s_z, b - 1)
                for t in range(H):
                    for k in range(H):
                        last = pe.matmul(ps_b[:, t * P:(t + 1) * P], adjT[c % 2][:, k, t * P:(t + 1) * P],
                                         pq[c % 2][:, k, 1:3, :].rearrange("p a d -> p (a d)"),
                                         start=(k == 0), stop=(k == H - 1))
                last.then_inc(s_sum_ps, 1)

            def look_up(b, c, f):
                if f == 2:
                    wait(pe, s_acc0, b + 1)
                elif f > 2:
                    wait(pe, s_acc, (MAIN - 1) * b + f - 2)
                else:
                    wait(pe, s_acc, (MAIN - 1) * (b - 1) + MAIN - 2 + f)
                if f == 0:
                    wait(pe, s_tabT, TFILLS * (b + 1))
                    wait(pe, s_hot, FILLS * (b + 1))
                for r in range(2 * (f // 2), min(2 * (f // 2) + 2, R)):
                    for j in range(2):
                        tile = slice(S * (2 * (f % 2) + j), S * (2 * (f % 2) + j + 1))
                        last = pe.matmul(ps_main[f % 2][:, j, r % 2, :], tableT[c % 2][tile, r, :], hot[c % 2][tile, r, :],
                                         start=True, stop=True)
                last.then_inc(s_round, 1)

            def ms_transposes(b, c):
                wait(pe, s_std, b + 1)
                for t in range(H):
                    last = pe.transpose(ps_b[:, t * P:(t + 1) * P], ms[c % 2][:, t].rearrange("p a d -> p (a d)"), ident[:])
                last.then_inc(s_msT_ps, 1)

            def z_nodes(b, c, has):
                wait(pe, s_z, b)
                if "M" in has:
                    wait(pe, s_msT, b + 2)
                wait(pe, s_fold, 2 * (b + 1))
                for t in range(H):
                    zt = ps_b[:, t * J * D:(t + 1) * J * D]
                    pe.matmul(zt, xT[c % 4][:, t, 0:P], w_x[:].rearrange("d j o -> d (j o)"), start=True, stop=False)
                    pe.matmul(zt, msT[c % 2][:, t, :], w_ms[:].rearrange("d j o -> d (j o)"), start=False, stop=False)
                    last = pe.matmul(zt, best[c % 2][:, t * P:(t + 1) * P], w_mx[:].rearrange("d j o -> d (j o)"),
                                     start=False, stop=True)
                last.then_inc(s_z_ps, 1)

            def one_step(s, c, has):
                p, q, m, n = s, s - 1, s - 2, s - 3
                if at(s, 1):
                    pe.wait_ge(s_signs, 1)
                if at(s, 3):
                    pe.wait_ge(s_setup, SET_UP)
                for r in range(MAIN):
                    if "M" in has:
                        look_up(m, c - 2, r)
                    if "P" in has and r == 0:
                        adj_transposes(p, c)
                    if "Q" in has and r % 2 == 0:
                        if r == 0:
                            wait(pe, s_mask, s)
                        hot_rows(q, c - 1, r // 2)
                    if "M" in has and r == 2:
                        wait(pe, s_uv, s - 1)
                        ms_transposes(m, c - 2)
                    if "P" in has and r == 2:
                        x_transposes(p, c)
                    if "Z" in has and r == 3:
                        z_nodes(n, c - 3, has)
                    if "Q" in has and r in (3, 5, 8, 10):
                        f = (3, 5, 8, 10).index(r)
                        if f == 0:
                            wait(pe, s_tab, K * s)
                        table_transposes(q, c - 1, f, has)
                    if "P" in has and r == 4:
                        q_rows(p, c)
                    if "P" in has and r == 6:
                        pq_nodes(p, c)
                    if "Q" in has and r == 11:
                        neighbour_sums(q, c - 1, has)

            pe.wait_ge(s_setup, 3)
            steps(pe, one_step)

        @block.scalar
        def _(act):
            def adjT_copy(b, c):
                wait(act, s_adjT_ps, b + 1)
                wait(act, s_sum_ps, b - 1)
                wait(act, s_mask, b - 1)
                nc.scalar.activation(adjT[c % 2][:].rearrange("p k n -> p (k n)"), ps_a[:], ACT.Copy).then_inc(s_adjT, 1)

            def xT_copy(b, c):
                wait(act, s_xT_ps, b + 1)
                wait(act, s_z_ps, b - 3)
                nc.scalar.activation(xT[c % 4][0:D, :, 0:P], ps_a[0:D, 0:H * P].rearrange("p (t m) -> p t m", t=H),
                                     ACT.Copy).then_inc(s_xT, 1)

            def pq_copy(b, c):
                wait(act, s_pq_ps, b + 1)
                wait(act, s_sum_ps, b - 1)
                wait(act, s_stat, STATS * (b - 1))
                src = ps_a[:, 0:H * P].rearrange("p (t a d) -> p t a d", t=H, a=2)
                nc.scalar.activation(pq[c % 2][:, :, 0:2, :], src, ACT.Copy).then_inc(s_p, 1)
                nc.scalar.activation(pq[c % 2][:, :, 2, :], src[:, :, 1, :], ACT.Square).then_inc(s_pq, 1)

            def hot_copy(b, c, f):
                wait(act, s_hot_ps, FILLS * b + f + 1)
                if f == 0:
                    wait(act, s_round, MAIN * (b - 1))
                n = min(2, R - 2 * f)
                nc.scalar.activation(hot[c % 2][:, 2 * f:2 * f + n, :], ps_hot[(c + f) % 2][:, 0:n, :], ACT.Relu,
                                     bias=hot_bias[:, 0:1]).then_inc(s_hot, 1)

            def tableT_copy(b, c, f):
                wait(act, s_tabT_ps, TFILLS * b + f + 1)
                n = min(4, R - 4 * f)
                nc.scalar.activation(tableT[c % 2][:, 4 * f:4 * f + n, :],
                                     ps_a[:, 0:n * P].rearrange("p (r m) -> p r m", m=P), ACT.Copy).then_inc(s_tabT, 1)

            def uv_copy(b, c):
                wait(act, s_sum_ps, b + 1)
                wait(act, s_stat, STATS * (b - 1))
                for t in range(H):
                    last = nc.scalar.activation(uv[c % 2][:, t].rearrange("p a d -> p (a d)"), ps_b[:, t * P:(t + 1) * P],
                                                ACT.Copy, scale=deg_inv[:, bass.ds(H * b + t, 1)])
                last.then_inc(s_uv, 1)

            def std_root(b, c):
                wait(act, s_stat, STATS * (b + 1))
                nc.scalar.activation(ms[c % 2][:, :, 1, :], var[c % 2][:], ACT.Sqrt, bias=eps_col[:, 0:1]) \
                    .then_inc(s_std, 1)

            def msT_copy(b, c):
                wait(act, s_msT_ps, b + 1)
                wait(act, s_z_ps, b - 1)
                nc.scalar.activation(msT[c % 2][:].rearrange("p t n -> p (t n)"), ps_b[:, 0:H * P], ACT.Copy) \
                    .then_inc(s_msT, 1)

            def start_acc(b, c):
                wait(act, s_round, MAIN * b + 1)
                wait(act, s_fold, 2 * (b - 1))
                nc.scalar.activation(acc[c % 2][:], ps_main[0][:], ACT.Copy).then_inc(s_acc0, 1)

            def z_copy(b, c):
                wait(act, s_z_ps, b + 1)
                wait(act, s_y, 3 * (b - 1))
                nc.scalar.activation(z[c % 2][:].rearrange("p t j o -> p (t j o)"), ps_b[:, 0:H * J * D], ACT.Copy) \
                    .then_inc(s_z, 1)

            def square_sums(b, c):
                wait(act, s_y, 3 * (b + 1))
                wait(act, s_root, b - 1)
                for t in range(H):
                    nc.scalar.activation(y_sq[:, t, :], y[c % 2][:, t, :], ACT.Square, accum_out=sumsq[:, c % 2, t:t + 1]) \
                        .then_inc(s_sq, 1)

            def norm_root(b, c):
                wait(act, s_sq, H * (b + 1))
                wait(act, s_rstd, b - 1)
                nc.scalar.activation(root[:, c % 2, :], sumsq[:, c % 2, :], ACT.Sqrt, bias=eps_col[:, 0:1],
                                     scale=1.0 / D).then_inc(s_root, 1)

            def logs(first, last, count):
                wait(act, s_deg, count)
                nc.scalar.activation(scaler[:, first:last, 0], deg1[:, first:last], ACT.Ln).then_inc(s_log, 1)

            def one_step(s, c, has):
                p, q, m, n = s, s - 1, s - 2, s - 3
                if at(s, 1):
                    logs(0, H * CH, DEG_FIRST)
                if at(s, 3):
                    logs(H * CH, H * B, DEG_ALL)
                for r in range(MAIN):
                    if "M" in has and r == 0:
                        start_acc(m, c - 2)
                    if "P" in has and r == 0:
                        adjT_copy(p, c)
                    if "Q" in has and r % 2 == 0:
                        hot_copy(q, c - 1, r // 2)
                    if "M" in has and r == 1:
                        std_root(m, c - 2)
                    if "P" in has and r == 2:
                        xT_copy(p, c)
                    if "M" in has and r == 2:
                        msT_copy(m, c - 2)
                    if "Z" in has and r == 3:
                        z_copy(n, c - 3)
                    if "Q" in has and r in (3, 5, 8, 10):
                        tableT_copy(q, c - 1, (3, 5, 8, 10).index(r))
                    if "P" in has and r == 6:
                        pq_copy(p, c)
                    if "Z" in has and r == 7:
                        square_sums(n, c - 3)
                    if "Z" in has and r == 8:
                        norm_root(n, c - 3)
                    if "Q" in has and r == 11:
                        uv_copy(q, c - 1)

            act.wait_ge(s_const, 16 * CONST_LOADS)
            act.wait_ge(s_fill, FILLED)
            nc.scalar.activation(sign[:], sign_f[:], ACT.Copy).then_inc(s_signs, 1)
            steps(act, one_step)

        @block.vector
        def _(dve):
            def table_step(b, c, i):
                if i == 0:
                    wait(dve, s_q_ps, b + 1)
                    wait(dve, s_tabT_ps, TFILLS * (b - 1))
                wait(dve, s_tab, K * b + i)
                low = table[c % 2][:, :, 0:1 << i]
                node = ps_b[:, 0:H * PAD].rearrange("p (g i) -> p g i", i=K)[:, :, i:i + 1].to_broadcast([P, G, 1 << i])
                nc.vector.tensor_tensor(table[c % 2][:, :, 1 << i:2 << i], low, node, ALU.max).then_inc(s_tab, 1)

            def take_round(b, c, r):
                wait(dve, s_round, MAIN * b + r + 1)
                if r == 1:
                    wait(dve, s_acc0, b + 1)
                else:
                    wait(dve, s_acc, (MAIN - 1) * b + r - 1)
                n = min(2, R - 2 * (r // 2))
                a = acc[c % 2][:, :, 0:n, :]
                nc.vector.tensor_tensor(a, ps_main[r % 2][:, :, 0:n, :], a, ALU.max).then_inc(s_acc, 1)

            def fold(b, c):
                wait(dve, s_acc, (MAIN - 1) * (b + 1))
                wait(dve, s_z_ps, b - 1)
                wait(dve, s_fold, 2 * b)
                a = acc[c % 2]
                nc.vector.tensor_tensor(folded[:], a[:, 0], a[:, 1], ALU.max).then_inc(s_fold, 1)
                wait(dve, s_fold, 2 * b + 1)
                nc.vector.tensor_tensor(best[c % 2][:], folded[:, 0, :], folded[:, 1, :], ALU.max).then_inc(s_fold, 1)

            def norm_inverse(b, c):
                wait(dve, s_root, b + 1)
                wait(dve, s_res, b - 1)
                nc.vector.reciprocal(rstd[:, c % 2, :], root[:, c % 2, :]).then_inc(s_rstd, 1)

            done = [0]

            def degree_chunk(c):
                wait(dve, s_all[c % 2], 16 * (c // 2 + 1))
                nc.vector.tensor_reduce(deg[:, H * CH * c:H * CH * (c + 1)], adj_all[:, c % 2].rearrange("p b t m -> p (b t) m"),
                                        AX.X, ALU.add).then_inc(s_deg, 1)
                done[0] += 1

            def degree_small(a, b):
                for out_, op in ((deg1, lambda: nc.vector.tensor_scalar(deg1[:, a:b], deg[:, a:b], 1.0, None, ALU.add)),
                                 (deg_safe, lambda: nc.vector.tensor_scalar(deg_safe[:, a:b], deg[:, a:b], 1.0, None, ALU.max)),
                                 (deg_inv, lambda: nc.vector.reciprocal(deg_inv[:, a:b], deg_safe[:, a:b])),
                                 (deg_part, lambda: nc.vector.tensor_tensor(deg_part[:, a:b], deg[:, a:b], deg_inv[:, a:b],
                                                                            ALU.mult))):
                    dve.wait_ge(s_deg, done[0])
                    op().then_inc(s_deg, 1)
                    done[0] += 1

            def inverse_logs(a, b, n):
                dve.wait_ge(s_log, 3 * n + 1)
                nc.vector.tensor_scalar(scaler[:, a:b, 1], scaler[:, a:b, 0], EPS, None, ALU.max).then_inc(s_log, 1)
                dve.wait_ge(s_log, 3 * n + 2)
                nc.vector.reciprocal(scaler[:, a:b, 1], scaler[:, a:b, 1]).then_inc(s_log, 1)

            setups = [0]

            def link(ins):
                setups[0] += 1
                ins.then_inc(s_setup, 1)
                dve.wait_ge(s_setup, setups[0])

            def setup_weights():
                dve.wait_ge(s_const, 16 * CONST_LOADS)
                dve.wait_ge(s_fill, FILLED)
                dve.wait_ge(s_setup_pe, 1)
                link(nc.vector.tensor_copy(w_pT[:], ps_b[0:D, 0:D + 1]))
                link(nc.vector.tensor_tensor(w_sum[:], w_fold[:, 0], w_fold[:, 1], ALU.add))
                dve.wait_ge(s_setup_pe, 2)
                link(nc.vector.tensor_copy(w_x[:], ps_b[0:D + 1, 0:J * D].rearrange("d (j o) -> d j o", j=J)))
                link(nc.vector.tensor_tensor(w_x0[0:D, :], w_x0[0:D, :], ident[0:D, 0:D], ALU.add))
                link(nc.vector.tensor_tensor(w_x[:, 0, :], w_x[:, 0, :], w_x0[:], ALU.add))
                link(nc.vector.tensor_scalar(w_mx[D:2 * D], w_mx[D:2 * D], -1.0, None, ALU.mult))
                for i, w in enumerate((w_x, w_ms, w_mx)):
                    k = w.shape[0]
                    link(nc.vector.tensor_scalar(w[:, 1, :], w[:, 1, :], 1.0 / AVG_D_LOG, None, ALU.mult))
                    link(nc.vector.tensor_scalar(w[:, 2, :], w[:, 2, :], AVG_D_LOG, None, ALU.mult))
                    link(nc.vector.tensor_reduce(w_mean[0:k, i, :], w[:], AX.X, ALU.add))
                    link(nc.vector.tensor_scalar(w_mean[0:k, i, :], w_mean[0:k, i, :], 1.0 / D, None, ALU.mult))
                    link(nc.vector.tensor_tensor(w[:], w[:], w_mean[0:k, i, :].unsqueeze(2).to_broadcast([k, J, D]),
                                                 ALU.subtract))

            def one_step(s, c, has):
                p, q, m, n = s, s - 1, s - 2, s - 3
                if at(s, 1):
                    degree_chunk(0)
                    degree_small(0, H * CH)
                    inverse_logs(0, H * CH, 0)
                for r in range(MAIN):
                    if "M" in has and r:
                        take_round(m, c - 2, r)
                    if "P" in has and 5 <= r < 5 + K:
                        table_step(p, c, r - 5)
                    if "Z" in has and r == 9:
                        norm_inverse(n, c - 3)
                    if at(s, 2) and r % 2 == 0 and 2 <= r:
                        degree_chunk(r // 2)
                        if r // 2 == 6:
                            degree_chunk(7)
                            degree_small(H * CH, H * B)
                    if at(s, 3) and r == 4:
                        inverse_logs(H * CH, H * B, 1)
                if "M" in has:
                    fold(m, c - 2)

            setup_weights()
            steps(dve, one_step)

        @block.gpsimd
        def _(pool):
            fills = [(w_pq[D:D + 1, D:2 * D], 0.0), (eps_col[:], EPS),
                     (table[0][:, :, 0:1], EMPTY), (table[1][:, :, 0:1], EMPTY)]
            for i in range(4):
                fills += [(xT[i][0:D, :, P:PAD], 0.0), (xT[i][D:D + 1], 1.0)]
            for i, (dst, value) in enumerate(fills):
                wait(pool, s_fill, i)
                nc.gpsimd.memset(dst, value).then_inc(s_fill, 1)
            pool.wait_ge(s_fill, len(fills))
            pool.wait_ge(s_const, 16 * CONST_LOADS)
            nc.gpsimd.tensor_scalar(w_qq[:, D:2 * D], w_qq[:, 0:D], -1.0, None, ALU.mult).then_inc(s_fill, 1)
            assert len(fills) + 1 == FILLED

            def neighbours(b, c):
                wait(pool, s_adjT, b + 1)
                wait(pool, s_hot_ps, FILLS * (b - 1))
                pool.sem_inc(s_go_mask, 1)
                nc.gpsimd.tensor_scalar(mask[c % 2][:], adjT[c % 2][:], 0.0, None, ALU.is_gt).then_inc(s_mask, 1)

            def statistics(b, c):
                wait(pool, s_uv, b + 1)
                wait(pool, s_msT_ps, b - 1)
                wait(pool, s_std, b - 1)
                u, v = uv[c % 2][:, :, 0, :], uv[c % 2][:, :, 1, :]
                p, mean = pq[c % 2][:, :, 0, :], ms[c % 2][:, :, 0, :]
                part = deg_part[:, bass.ds(H * b, H)].unsqueeze(2).to_broadcast([P, H, D])
                tensors = ((pool_a[:], p, part, ALU.mult), (mean, pool_a[:], u, ALU.add),
                           (pool_a[:], p, pool_a[:], ALU.subtract), (pool_b[:], mean, u, ALU.add),
                           (pool_b[:], pool_a[:], pool_b[:], ALU.mult), (pool_c[:], u, u, ALU.mult),
                           (pool_c[:], v, pool_c[:], ALU.subtract), (pool_c[:], pool_c[:], pool_b[:], ALU.add))
                for i, (dst, a, b_, op) in enumerate(tensors):
                    wait(pool, s_stat, STATS * b + i)
                    nc.gpsimd.tensor_tensor(dst, a, b_, op).then_inc(s_stat, 1)
                wait(pool, s_stat, STATS * b + len(tensors))
                pool.sem_inc(s_go_var, 1)
                nc.gpsimd.tensor_scalar(var[c % 2][:], pool_c[:], 0.0, None, ALU.max).then_inc(s_stat, 1)

            def scaled_sum(b, c):
                wait(pool, s_z, b + 1)
                wait(pool, s_y, 3 * b)
                scale = scaler[:, bass.ds(H * b, H), :].unsqueeze(3).to_broadcast([P, H, 2, D])
                nc.gpsimd.tensor_tensor(zs[:], z[c % 2][:, :, 1:3, :], scale, ALU.mult).then_inc(s_y, 1)
                wait(pool, s_y, 3 * b + 1)
                nc.gpsimd.tensor_tensor(y1[:], z[c % 2][:, :, 0, :], zs[:, :, 0, :], ALU.add).then_inc(s_y, 1)
                wait(pool, s_y, 3 * b + 2)
                wait(pool, s_res, b - 1)
                nc.gpsimd.tensor_tensor(y[c % 2][:], y1[:], zs[:, :, 1, :], ALU.add).then_inc(s_y, 1)

            def normalise(b, c):
                wait(pool, s_rstd, b + 1)
                wait(pool, s_out[c % 2], half(b, c) - 16)
                nc.gpsimd.tensor_tensor(result[c % 2][:], y[c % 2][:], rstd[:, c % 2, :].unsqueeze(2).to_broadcast([P, H, D]),
                                        ALU.mult).then_inc(s_res, 1)

            def one_step(s, c, has):
                if "P" in has:
                    neighbours(s, c)
                if at(s, 3):
                    pool.wait_ge(s_log, 6)
                    pool.wait_ge(s_deg, DEG_ALL)
                if "Z" in has:
                    scaled_sum(s - 3, c - 3)
                    normalise(s - 3, c - 3)
                if "Q" in has:
                    if at(s, 1):
                        pool.wait_ge(s_deg, DEG_FIRST)
                    statistics(s - 1, c - 1)

            steps(pool, one_step)


_INS = ["x", "adj", "L0_gnn_W_pre", "L0_gnn_b_pre", "L0_gnn_W_post", "L0_gnn_b_post"]


def kernel(**inputs):
    import numpy as _np
    import concourse.bacc as _bacc
    from concourse import mybir as _mybir
    from concourse.bass_utils import run_bass_kernel_spmd as _run

    nc = _bacc.Bacc("TRN2", target_bir_lowering=False, num_devices=1)
    arrays, args = {}, []
    given = [(name, inputs[name]) for name in _INS] + list(zip(("ident", "sign", "bias"), constants()))
    for name, a in given:
        a = _np.ascontiguousarray(a)
        arrays[f"in_{name}_dram"] = a
        args.append(nc.dram_tensor(f"in_{name}_dram", a.shape, _mybir.dt.from_np(a.dtype), kind="ExternalInput").ap())
    args.append(nc.dram_tensor("out_0_dram", (B, N, D), F32, kind="ExternalOutput").ap())
    pna_layer(nc, *args)
    r = _run(nc, [arrays], core_ids=[0])
    return r.results[0]["out_0_dram"]
```

```python
from contextlib import ExitStack

import numpy as np

import concourse.bass as bass
from concourse import mybir

F32 = mybir.dt.float32
F32R = mybir.dt.float32r
BF16 = mybir.dt.bfloat16
ALU = mybir.AluOpType
ACT = mybir.ActivationFunctionType
AX = mybir.AxisListType

P = 128
B, N, D = 32, 256, 64
H = N // P
K = 5
S = 2 ** K
ROWS = 2 * S
TILES = P // ROWS
GH = -(-P // K)
G = H * GH
R = G // TILES
PAD = GH * K
RH = R // H
FILLS = R // 2
TFILLS = -(-R // 4)
J = 3
AVG_D_LOG = 4.86
EPS = 1e-05
EMPTY = -1e9
CH = 4
CHUNKS = B // CH
T_SLOTS = (1, 3, 4, 5, 7, 8, 9)
STATS = 9
STORE_LAG = 6
DEG_SMALL = 4
LOOP_FIRST, UNROLL = 8, 4
LOOP_TRIPS = (B - LOOP_FIRST) // UNROLL


def constants():
    sign = np.zeros((P, RH, TILES, 2, S), np.float32)
    for g in range(GH):
        for i in range(min(K, P - K * g)):
            for s in range(S):
                sign[K * g + i, g // TILES, g % TILES, :, s] = 1.0 if s >> i & 1 else -1.0
    bias = np.array([[1.0 - bin(s % S).count("1")] for s in range(P)], np.float32)
    return np.eye(P, dtype=np.float32), sign.reshape(P, -1), bias


def pna_layer(nc, x, adj, w_pre, b_pre, w_post, b_post, ident_in, sign_in, bias_in, out):
    with ExitStack() as ctx:
        def sb(name, shape, dt=F32):
            return ctx.enter_context(nc.sbuf_tensor(name, shape, dt))

        def sem(name):
            return ctx.enter_context(nc.semaphore(name))

        ident = sb("ident", [P, P])
        sign_f = sb("sign_f", [P, RH, P])
        sign = sb("sign", [P, RH, P], BF16)
        hot_bias = sb("hot_bias", [P, 1])
        w_pq = sb("w_pq", [D + 1, 2 * D])
        w_qq = sb("w_qq", [D, 2 * D])
        w_pT = sb("w_pT", [D, D + 1])
        w_fold = sb("w_fold", [D, 2, J, D])
        w_sum = sb("w_sum", [D, J, D])
        w_x = sb("w_x", [D + 1, J, D])
        w_x0 = sb("w_x0", [D + 1, D])
        w_ms = sb("w_ms", [P, J, D])
        w_mx = sb("w_mx", [P, J, D])
        w_mean = sb("w_mean", [P, 3, J])
        adj_all = sb("adj_all", [P, 2, CH, H, N])
        deg = sb("deg", [P, B * H])
        deg1 = sb("deg1", [P, B * H])
        deg_safe = sb("deg_safe", [P, B * H])
        deg_inv = sb("deg_inv", [P, B * H])
        deg_part = sb("deg_part", [P, B * H])
        scaler = sb("scaler", [P, B * H, 2])
        x_in = [sb(f"x_in{i}", [P, H, D]) for i in range(2)]
        adj_in = [sb(f"adj_in{i}", [P, H, N]) for i in range(2)]
        adjT = [sb(f"adjT{i}", [P, H, N]) for i in range(2)]
        mask = [sb(f"mask{i}", [P, H, N], BF16) for i in range(2)]
        xT = [sb(f"xT{i}", [D + 1, H, PAD]) for i in range(4)]
        pq = [sb(f"pq{i}", [P, H, 3, D]) for i in range(2)]
        table = [sb(f"table{i}", [P, G, S]) for i in range(2)]
        parts = [sb(f"parts{i}", [P, G, 2, S]) for i in range(2)]
        tableT = [sb(f"tableT{i}", [P, R, P], F32R) for i in range(2)]
        hot = [sb(f"hot{i}", [P, R, N], F32R) for i in range(2)]
        acc = [sb(f"acc{i}", [P, 2, 2, N]) for i in range(2)]
        folded = sb("folded", [P, 2, N])
        best = [sb(f"best{i}", [P, N]) for i in range(2)]
        uv = [sb(f"uv{i}", [P, H, 2, D]) for i in range(2)]
        pool_a = sb("pool_a", [P, H, D])
        pool_b = sb("pool_b", [P, H, D])
        pool_c = sb("pool_c", [P, H, D])
        var = [sb(f"var{i}", [P, H, D]) for i in range(2)]
        ms = [sb(f"ms{i}", [P, H, 2, D]) for i in range(2)]
        msT = [sb(f"msT{i}", [P, H, P]) for i in range(4)]
        z = [sb(f"z{i}", [P, H, J, D]) for i in range(2)]
        zs = sb("zs", [P, H, 2, D])
        y1 = sb("y1", [P, H, D])
        y = [sb(f"y_out{i}", [P, H, D]) for i in range(2)]
        y_sq = sb("y_sq", [P, H, D])
        sumsq = sb("sumsq", [P, 2, H])
        root = sb("root", [P, 2, H])
        rstd = sb("rstd", [P, 2, H])
        result = [sb(f"result{i}", [P, H, D]) for i in range(2)]
        eps_col = sb("eps_col", [P, 1])

        ps_main = [ctx.enter_context(nc.psum_tensor(f"ps_main{i}", [P, 2, 2, N], F32)) for i in range(2)]
        ps_hot = [ctx.enter_context(nc.psum_tensor(f"ps_hot{i}", [P, 2, N], F32)) for i in range(2)]
        ps_a = ctx.enter_context(nc.psum_tensor("ps_a", [P, 4 * P], F32))
        ps_b = ctx.enter_context(nc.psum_tensor("ps_b", [P, 4 * P], F32))

        s_const = sem("const_loaded")
        s_x = [sem(f"x_loaded{i}") for i in range(2)]
        s_adj = [sem(f"adj_loaded{i}") for i in range(2)]
        s_all = [sem(f"adj_chunk_loaded{i}") for i in range(2)]
        s_out = [sem(f"stored{i}") for i in range(2)]
        s_fill = sem("fills_done")
        s_setup = sem("setup_step")
        s_setup_pe = sem("setup_pe")
        s_signs = sem("signs_ready")
        s_deg = sem("deg_step")
        s_log = sem("log_ready")
        s_adjT_ps = sem("adjT_in_psum")
        s_xT_ps = sem("xT_in_psum")
        s_q_ps = sem("q_in_psum")
        s_pq_ps = sem("pq_in_psum")
        s_tabT_ps = sem("tableT_in_psum")
        s_hot_ps = sem("hot_in_psum")
        s_sum_ps = sem("sums_in_psum")
        s_msT_ps = sem("msT_in_psum")
        s_z_ps = sem("z_in_psum")
        s_round = sem("round_in_psum")
        s_adjT = sem("adjT_ready")
        s_xT = sem("xT_ready")
        s_p = sem("p_ready")
        s_pq = sem("pq_ready")
        s_tabT = sem("tableT_ready")
        s_hot = sem("hot_ready")
        s_uv = sem("uv_ready")
        s_std = sem("std_ready")
        s_msT = sem("msT_ready")
        s_acc0 = sem("acc_started")
        s_z = sem("z_copied")
        s_sq = sem("sumsq_ready")
        s_root = sem("root_ready")
        s_tab = sem("table_step")
        s_upper = sem("upper_parts_ready")
        s_acc = sem("acc_step")
        s_fold = sem("fold_step")
        s_rstd = sem("rstd_ready")
        s_go_x = sem("go_x_transposes")
        s_go_mask = sem("go_mask")
        s_go_var = sem("go_var")
        s_mask = sem("mask_ready")
        s_lower = sem("lower_parts_ready")
        s_stat = sem("stats_step")
        s_y = sem("y_step")
        s_res = sem("result_ready")

        def wait(eng, s, value):
            if not isinstance(value, int) or value > 0:
                eng.wait_ge(s, value)

        def half(b, c):
            return 8 * b + (16 - 8 * (c % 2))

        def at(s, n):
            return isinstance(s, int) and s == n

        def steps(eng, one_step):
            def has(s):
                return "".join(n for i, n in enumerate("PQMZ") if 0 <= s - i < B)
            for s in range(LOOP_FIRST):
                one_step(s, s % 4, has(s))
            with eng.Fori(0, LOOP_TRIPS) as i:
                for u in range(UNROLL):
                    one_step(UNROLL * i + (LOOP_FIRST + u), u, "PQMZ")
            for s in range(B, B + 3):
                one_step(s, s % 4, has(s))

        x_rows = x.rearrange("b (p t) d -> b p t d", t=H)
        adj_rows = adj.rearrange("b (p t) m -> b p t m", t=H)
        out_rows = out.rearrange("b (p t) d -> b p t d", t=H)
        post = w_post[D:, :].rearrange("(j k d) o -> k d j o", j=J, k=4)
        CONST_LOADS = 15
        FILLED = 13
        SET_UP = 21

        DEG_FIRST = 1 + DEG_SMALL
        DEG_ALL = CHUNKS + 2 * DEG_SMALL

        block = ctx.enter_context(nc.Block())

        @block.sync
        def _(sp):
            def load(b, c):
                wait(sp, s_adjT_ps, b - 1)
                sp.dma_start(adj_in[c % 2][:], adj_rows[b]).then_inc(s_adj[c % 2], 16)
                wait(sp, s_xT_ps, b - 1)
                sp.dma_start(x_in[c % 2][:], x_rows[b]).then_inc(s_x[c % 2], 16)

            loads = [
                (ident[:], ident_in), (sign_f[:].rearrange("p r c -> p (r c)"), sign_in), (hot_bias[:], bias_in),
                (w_pq[0:D, 0:D], w_pre[0:D, :]), (w_pq[D:D + 1, 0:D], b_pre.rearrange("(a d) -> a d", a=1)),
                (w_pq[0:D, D:2 * D], w_pre[D:2 * D, :]), (w_qq[:, 0:D], w_pre[D:2 * D, :]),
                (w_x0[0:D, :], w_post[0:D, :]), (w_x0[D:D + 1, :], b_post.rearrange("(a d) -> a d", a=1)),
                (w_ms[0:D, :, :], post[0]), (w_ms[D:2 * D, :, :], post[3]),
                (w_mx[0:D, :, :], post[1]), (w_mx[D:2 * D, :, :], post[2]),
                (w_fold[:, 0, :, :], post[1]), (w_fold[:, 1, :, :], post[2]),
            ]
            assert len(loads) == CONST_LOADS
            sp.dma_start(*loads[0]).then_inc(s_const, 16)
            load(0, 0)
            for dst, src in loads[1:]:
                sp.dma_start(dst, src).then_inc(s_const, 16)
            load(1, 1)
            for c in range(CHUNKS):
                if c >= 2:
                    sp.wait_ge(s_deg, 1 if c == 2 else 1 + DEG_SMALL + c - 2)
                sp.dma_start(adj_all[:, c % 2], adj_rows[CH * c:CH * c + CH].rearrange("b p t m -> p b t m")) \
                    .then_inc(s_all[c % 2], 16)
                if c in (1, 3):
                    load((c + 3) // 2, (c + 3) // 2)

            def store(b, c):
                wait(sp, s_res, b + 1)
                sp.dma_start(out_rows[b], result[c % 2][:]).then_inc(s_out[c % 2], 16)

            for b in range(UNROLL, 2 * UNROLL):
                load(b, b % 4)
                if b >= STORE_LAG:
                    store(b - STORE_LAG, (b - STORE_LAG) % 4)
            with sp.Fori(0, B // UNROLL - 2) as i:
                for u in range(UNROLL):
                    load(UNROLL * i + (2 * UNROLL + u), u)
                    store(UNROLL * i + (2 * UNROLL + u - STORE_LAG), (u - STORE_LAG) % 4)
            for b in range(B - STORE_LAG, B):
                store(b, b % 4)
            for c in range(2):
                sp.wait_ge(s_out[c], 16 * B // 2)

        @block.tensor
        def _(pe):
            wait(pe, s_const, 16 * CONST_LOADS)
            wait(pe, s_fill, FILLED)
            pe.transpose(ps_b[0:D, 0:D + 1], w_pq[:, 0:D], ident[0:D + 1, 0:D + 1]).then_inc(s_setup_pe, 1)
            pe.wait_ge(s_setup, 2)
            pe.matmul(ps_b[0:D + 1, 0:J * D], w_pT[:], w_sum[:].rearrange("d j o -> d (j o)"), start=True, stop=True) \
                .then_inc(s_setup_pe, 1)

            def adj_transposes(b, c):
                wait(pe, s_adj[c % 2], half(b, c))
                wait(pe, s_pq, b)
                wait(pe, s_tabT, TFILLS * (b - 1))
                for k in range(H):
                    for t in range(H):
                        last = pe.transpose(ps_a[:, (k * H + t) * P:(k * H + t + 1) * P],
                                            adj_in[c % 2][:, t, k::H], ident[:])
                last.then_inc(s_adjT_ps, 1)

            def x_transposes(b, c):
                wait(pe, s_x[c % 2], half(b, c))
                wait(pe, s_adjT, b + 1)
                wait(pe, s_tabT, TFILLS * (b - 1) + 1)
                pe.sem_inc(s_go_x, 1)
                for t in range(H):
                    last = pe.transpose(ps_a[0:D, t * P:(t + 1) * P], x_in[c % 2][:, t, :], ident[:])
                last.then_inc(s_xT_ps, 1)

            def q_rows(b, c):
                wait(pe, s_xT, b + 1)
                wait(pe, s_msT, b - 1)
                wait(pe, s_uv, b)
                wait(pe, s_z, b - 2)
                pe.matmul(ps_b[:, 0:H * PAD], w_qq[:], xT[c % 4][0:D].rearrange("d t m -> d (t m)"),
                          start=True, stop=True).then_inc(s_q_ps, 1)

            def pq_nodes(b, c):
                wait(pe, s_xT, b + 1)
                wait(pe, s_tabT, TFILLS * (b - 1) + 4)
                for t in range(H):
                    last = pe.matmul(ps_a[:, t * P:(t + 1) * P], xT[c % 4][:, t, 0:P], w_pq[:], start=True, stop=True)
                last.then_inc(s_pq_ps, 1)

            def hot_rows(b, c, f):
                wait(pe, s_hot, FILLS * b + f - 1)
                for r in range(2 * f, 2 * f + 2):
                    last = pe.matmul(ps_hot[(c + f) % 2][:, r % 2, :], sign[:, r % RH, :], mask[c % 2][:, r // RH, :],
                                     start=True, stop=True)
                last.then_inc(s_hot_ps, 1)

            def table_transposes(b, c, f, has):
                if f == 0:
                    wait(pe, s_lower, b + 1)
                if "P" in has:
                    if f == 0:
                        wait(pe, s_adjT, b + 2)
                    elif f == 1:
                        wait(pe, s_xT, b + 2)
                    elif f == 4:
                        wait(pe, s_pq, b + 2)
                wait(pe, s_tabT, TFILLS * b + f)
                for r in range(4 * f, min(4 * f + 4, R)):
                    last = pe.transpose(ps_a[:, (r % 4) * P:(r % 4 + 1) * P],
                                        parts[c % 2][:, TILES * r:TILES * r + TILES].rearrange("p g a s -> p (g a s)"),
                                        ident[:])
                last.then_inc(s_tabT_ps, 1)

            def neighbour_sums(b, c):
                wait(pe, s_adjT, b + 1)
                wait(pe, s_pq, b + 1)
                wait(pe, s_msT, b)
                wait(pe, s_tab, K * (b + 1))
                for t in range(H):
                    for k in range(H):
                        last = pe.matmul(ps_b[:, t * P:(t + 1) * P], adjT[c % 2][:, k, t * P:(t + 1) * P],
                                         pq[c % 2][:, k, 1:3, :].rearrange("p a d -> p (a d)"),
                                         start=(k == 0), stop=(k == H - 1))
                last.then_inc(s_sum_ps, 1)

            def look_up(b, c, f):
                if f == 2:
                    wait(pe, s_acc0, b + 1)
                elif f > 2:
                    wait(pe, s_acc, (FILLS - 1) * b + f - 2)
                else:
                    wait(pe, s_acc, (FILLS - 1) * (b - 1) + FILLS - 2 + f)
                if f == 0:
                    wait(pe, s_tabT, TFILLS * (b + 1))
                    wait(pe, s_hot, FILLS * (b + 1))
                for r in range(2 * f, 2 * f + 2):
                    for j in range(TILES):
                        rows = slice(ROWS * j, ROWS * (j + 1))
                        last = pe.matmul(ps_main[(c + f) % 2][:, j, r % 2, :], tableT[c % 2][rows, r, :],
                                         hot[c % 2][rows, r, :], start=True, stop=True)
                last.then_inc(s_round, 1)

            def ms_transposes(b, c, has):
                wait(pe, s_std, b + 1)
                if "P" in has:
                    wait(pe, s_tab, K * (b + 2))
                wait(pe, s_uv, b + 1)
                wait(pe, s_z, b - 1)
                for t in range(H):
                    last = pe.transpose(ps_b[:, t * P:(t + 1) * P], ms[c % 2][:, t].rearrange("p a d -> p (a d)"), ident[:])
                last.then_inc(s_msT_ps, 1)

            def z_nodes(b, c, has):
                wait(pe, s_z, b)
                wait(pe, s_msT, min(b + 2, B) if isinstance(b, int) else b + 2)
                if "Q" in has:
                    wait(pe, s_uv, b + 3)
                wait(pe, s_fold, 2 * (b + 1))
                for t in range(H):
                    zt = ps_b[:, t * J * D:(t + 1) * J * D]
                    pe.matmul(zt, xT[c % 4][:, t, 0:P], w_x[:].rearrange("d j o -> d (j o)"), start=True, stop=False)
                    pe.matmul(zt, msT[c % 4][:, t, :], w_ms[:].rearrange("d j o -> d (j o)"), start=False, stop=False)
                    last = pe.matmul(zt, best[c % 2][:, t * P:(t + 1) * P], w_mx[:].rearrange("d j o -> d (j o)"),
                                     start=False, stop=True)
                last.then_inc(s_z_ps, 1)

            def one_step(s, c, has):
                p, q, m, n = s, s - 1, s - 2, s - 3
                if at(s, 1):
                    pe.wait_ge(s_signs, 1)
                if at(s, 3):
                    pe.wait_ge(s_setup, SET_UP)
                for f in range(FILLS):
                    if "M" in has:
                        look_up(m, c - 2, f)
                    if "P" in has and f == 0:
                        adj_transposes(p, c)
                    if "Q" in has:
                        if f == 0:
                            neighbour_sums(q, c - 1)
                            wait(pe, s_mask, s)
                        hot_rows(q, c - 1, f)
                    if "Z" in has and f == 2:
                        z_nodes(n, c - 3, has)
                    if "P" in has and f == 2:
                        x_transposes(p, c)
                    if "P" in has and f == 4:
                        q_rows(p, c)
                    if "P" in has and f == 6:
                        pq_nodes(p, c)
                    if "Q" in has and f in T_SLOTS:
                        table_transposes(q, c - 1, T_SLOTS.index(f), has)
                    if "Q" in has and f == 11:
                        ms_transposes(q, c - 1, has)

            pe.wait_ge(s_setup, 3)
            steps(pe, one_step)

        @block.scalar
        def _(act):
            def adjT_copy(b, c):
                wait(act, s_adjT_ps, b + 1)
                wait(act, s_sum_ps, b - 1)
                wait(act, s_mask, b - 1)
                nc.scalar.activation(adjT[c % 2][:].rearrange("p k n -> p (k n)"), ps_a[:], ACT.Copy).then_inc(s_adjT, 1)

            def xT_copy(b, c):
                wait(act, s_xT_ps, b + 1)
                wait(act, s_z_ps, b - 3)
                nc.scalar.activation(xT[c % 4][0:D, :, 0:P], ps_a[0:D, 0:H * P].rearrange("p (t m) -> p t m", t=H),
                                     ACT.Copy).then_inc(s_xT, 1)

            def pq_copy(b, c):
                wait(act, s_pq_ps, b + 1)
                wait(act, s_sum_ps, b - 1)
                wait(act, s_stat, STATS * (b - 1))
                src = ps_a[:, 0:H * P].rearrange("p (t a d) -> p t a d", t=H, a=2)
                nc.scalar.activation(pq[c % 2][:, :, 0:2, :], src, ACT.Copy).then_inc(s_p, 1)
                nc.scalar.activation(pq[c % 2][:, :, 2, :], src[:, :, 1, :], ACT.Square).then_inc(s_pq, 1)

            def hot_copy(b, c, f):
                wait(act, s_hot_ps, FILLS * b + f + 1)
                if f == 0:
                    wait(act, s_round, FILLS * (b - 1))
                nc.scalar.activation(hot[c % 2][:, 2 * f:2 * f + 2, :], ps_hot[(c + f) % 2][:], ACT.Relu,
                                     bias=hot_bias[:, 0:1]).then_inc(s_hot, 1)

            def tableT_copy(b, c, f):
                wait(act, s_tabT_ps, TFILLS * b + f + 1)
                n = min(4, R - 4 * f)
                nc.scalar.activation(tableT[c % 2][:, 4 * f:4 * f + n, :],
                                     ps_a[:, 0:n * P].rearrange("p (r m) -> p r m", m=P), ACT.Copy).then_inc(s_tabT, 1)

            def uv_copy(b, c):
                wait(act, s_sum_ps, b + 1)
                wait(act, s_stat, STATS * (b - 1))
                for t in range(H):
                    last = nc.scalar.activation(uv[c % 2][:, t].rearrange("p a d -> p (a d)"), ps_b[:, t * P:(t + 1) * P],
                                                ACT.Copy, scale=deg_inv[:, bass.ds(H * b + t, 1)])
                last.then_inc(s_uv, 1)

            def std_root(b, c):
                wait(act, s_stat, STATS * (b + 1))
                nc.scalar.activation(ms[c % 2][:, :, 1, :], var[c % 2][:], ACT.Sqrt, bias=eps_col[:, 0:1]) \
                    .then_inc(s_std, 1)

            def msT_copy(b, c):
                wait(act, s_msT_ps, b + 1)
                wait(act, s_z_ps, b - 3)
                nc.scalar.activation(msT[c % 4][:].rearrange("p t n -> p (t n)"), ps_b[:, 0:H * P], ACT.Copy) \
                    .then_inc(s_msT, 1)

            def start_acc(b, c):
                wait(act, s_round, FILLS * b + 1)
                wait(act, s_fold, 2 * (b - 1))
                nc.scalar.activation(acc[c % 2][:], ps_main[c % 2][:], ACT.Copy).then_inc(s_acc0, 1)

            def z_copy(b, c):
                wait(act, s_z_ps, b + 1)
                wait(act, s_y, 3 * (b - 1))
                nc.scalar.activation(z[c % 2][:].rearrange("p t j o -> p (t j o)"), ps_b[:, 0:H * J * D], ACT.Copy) \
                    .then_inc(s_z, 1)

            def square_sums(b, c):
                wait(act, s_y, 3 * (b + 1))
                wait(act, s_root, b - 1)
                for t in range(H):
                    nc.scalar.activation(y_sq[:, t, :], y[c % 2][:, t, :], ACT.Square, accum_out=sumsq[:, c % 2, t:t + 1]) \
                        .then_inc(s_sq, 1)

            def norm_root(b, c):
                wait(act, s_sq, H * (b + 1))
                wait(act, s_rstd, b - 1)
                nc.scalar.activation(root[:, c % 2, :], sumsq[:, c % 2, :], ACT.Sqrt, bias=eps_col[:, 0:1],
                                     scale=1.0 / D).then_inc(s_root, 1)

            def logs(first, last, count):
                wait(act, s_deg, count)
                nc.scalar.activation(scaler[:, first:last, 0], deg1[:, first:last], ACT.Ln).then_inc(s_log, 1)

            def one_step(s, c, has):
                p, q, m, n = s, s - 1, s - 2, s - 3
                if at(s, 1):
                    logs(0, H * CH, DEG_FIRST)
                if at(s, 3):
                    logs(H * CH, H * B, DEG_ALL)
                for f in range(FILLS):
                    if "M" in has and f == 0:
                        start_acc(m, c - 2)
                    if "P" in has and f == 0:
                        adjT_copy(p, c)
                    if "Q" in has and f == 0:
                        uv_copy(q, c - 1)
                    if "Q" in has:
                        hot_copy(q, c - 1, f)
                    if "Z" in has and f == 2:
                        z_copy(n, c - 3)
                    if "P" in has and f == 2:
                        xT_copy(p, c)
                    if "P" in has and f == 6:
                        pq_copy(p, c)
                    if "Q" in has and f in T_SLOTS:
                        tableT_copy(q, c - 1, T_SLOTS.index(f))
                    if "Z" in has and f == 6:
                        square_sums(n, c - 3)
                    if "Z" in has and f == 7:
                        norm_root(n, c - 3)
                    if "Q" in has and f == 8:
                        std_root(q, c - 1)
                    if "Q" in has and f == 11:
                        msT_copy(q, c - 1)

            act.wait_ge(s_const, 16 * CONST_LOADS)
            act.wait_ge(s_fill, FILLED)
            nc.scalar.activation(sign[:], sign_f[:], ACT.Copy).then_inc(s_signs, 1)
            steps(act, one_step)

        @block.vector
        def _(dve):
            def table_step(b, c, i):
                if i == 0:
                    wait(dve, s_q_ps, b + 1)
                    wait(dve, s_lower, b - 1)
                wait(dve, s_tab, K * b + i)
                low = table[c % 2][:, :, 0:1 << i]
                node = ps_b[:, 0:H * PAD].rearrange("p (g i) -> p g i", i=K)[:, :, i:i + 1].to_broadcast([P, G, 1 << i])
                nc.vector.tensor_tensor(table[c % 2][:, :, 1 << i:2 << i], low, node, ALU.max).then_inc(s_tab, 1)

            def upper_parts(b, c):
                wait(dve, s_tab, K * (b + 1))
                wait(dve, s_tabT_ps, TFILLS * (b - 1))
                nc.vector.tensor_copy(parts[c % 2][:, :, 0, :].bitcast(F32R), table[c % 2][:]).then_inc(s_upper, 1)

            def take_round(b, c, r):
                wait(dve, s_round, FILLS * b + r + 1)
                if r == 1:
                    wait(dve, s_acc0, b + 1)
                else:
                    wait(dve, s_acc, (FILLS - 1) * b + r - 1)
                a = acc[c % 2][:]
                nc.vector.tensor_tensor(a, ps_main[(c + r) % 2][:], a, ALU.max).then_inc(s_acc, 1)

            def fold(b, c):
                wait(dve, s_acc, (FILLS - 1) * (b + 1))
                wait(dve, s_z_ps, b - 1)
                wait(dve, s_fold, 2 * b)
                a = acc[c % 2]
                nc.vector.tensor_tensor(folded[:], a[:, 0], a[:, 1], ALU.max).then_inc(s_fold, 1)
                wait(dve, s_fold, 2 * b + 1)
                nc.vector.tensor_tensor(best[c % 2][:], folded[:, 0, :], folded[:, 1, :], ALU.max).then_inc(s_fold, 1)

            def norm_inverse(b, c):
                wait(dve, s_root, b + 1)
                wait(dve, s_res, b - 1)
                nc.vector.reciprocal(rstd[:, c % 2, :], root[:, c % 2, :]).then_inc(s_rstd, 1)

            done = [0]

            def degree_chunk(c):
                wait(dve, s_all[c % 2], 16 * (c // 2 + 1))
                nc.vector.tensor_reduce(deg[:, H * CH * c:H * CH * (c + 1)], adj_all[:, c % 2].rearrange("p b t m -> p (b t) m"),
                                        AX.X, ALU.add).then_inc(s_deg, 1)
                done[0] += 1

            def degree_small(a, b):
                for out_, op in ((deg1, lambda: nc.vector.tensor_scalar(deg1[:, a:b], deg[:, a:b], 1.0, None, ALU.add)),
                                 (deg_safe, lambda: nc.vector.tensor_scalar(deg_safe[:, a:b], deg[:, a:b], 1.0, None, ALU.max)),
                                 (deg_inv, lambda: nc.vector.reciprocal(deg_inv[:, a:b], deg_safe[:, a:b])),
                                 (deg_part, lambda: nc.vector.tensor_tensor(deg_part[:, a:b], deg[:, a:b], deg_inv[:, a:b],
                                                                            ALU.mult))):
                    dve.wait_ge(s_deg, done[0])
                    op().then_inc(s_deg, 1)
                    done[0] += 1

            def inverse_logs(a, b, n):
                dve.wait_ge(s_log, 3 * n + 1)
                nc.vector.tensor_scalar(scaler[:, a:b, 1], scaler[:, a:b, 0], EPS, None, ALU.max).then_inc(s_log, 1)
                dve.wait_ge(s_log, 3 * n + 2)
                nc.vector.reciprocal(scaler[:, a:b, 1], scaler[:, a:b, 1]).then_inc(s_log, 1)

            setups = [0]

            def link(ins):
                setups[0] += 1
                ins.then_inc(s_setup, 1)
                dve.wait_ge(s_setup, setups[0])

            def setup_weights():
                dve.wait_ge(s_const, 16 * CONST_LOADS)
                dve.wait_ge(s_fill, FILLED)
                dve.wait_ge(s_setup_pe, 1)
                link(nc.vector.tensor_copy(w_pT[:], ps_b[0:D, 0:D + 1]))
                link(nc.vector.tensor_tensor(w_sum[:], w_fold[:, 0], w_fold[:, 1], ALU.add))
                dve.wait_ge(s_setup_pe, 2)
                link(nc.vector.tensor_copy(w_x[:], ps_b[0:D + 1, 0:J * D].rearrange("d (j o) -> d j o", j=J)))
                link(nc.vector.tensor_tensor(w_x0[0:D, :], w_x0[0:D, :], ident[0:D, 0:D], ALU.add))
                link(nc.vector.tensor_tensor(w_x[:, 0, :], w_x[:, 0, :], w_x0[:], ALU.add))
                link(nc.vector.tensor_scalar(w_mx[D:2 * D], w_mx[D:2 * D], -1.0, None, ALU.mult))
                for i, w in enumerate((w_x, w_ms, w_mx)):
                    k = w.shape[0]
                    link(nc.vector.tensor_scalar(w[:, 1, :], w[:, 1, :], 1.0 / AVG_D_LOG, None, ALU.mult))
                    link(nc.vector.tensor_scalar(w[:, 2, :], w[:, 2, :], AVG_D_LOG, None, ALU.mult))
                    link(nc.vector.tensor_reduce(w_mean[0:k, i, :], w[:], AX.X, ALU.add))
                    link(nc.vector.tensor_scalar(w_mean[0:k, i, :], w_mean[0:k, i, :], 1.0 / D, None, ALU.mult))
                    link(nc.vector.tensor_tensor(w[:], w[:], w_mean[0:k, i, :].unsqueeze(2).to_broadcast([k, J, D]),
                                                 ALU.subtract))

            def one_step(s, c, has):
                p, q, m, n = s, s - 1, s - 2, s - 3
                if at(s, 1):
                    degree_chunk(0)
                    degree_small(0, H * CH)
                    inverse_logs(0, H * CH, 0)
                for r in range(FILLS):
                    if "M" in has and r:
                        take_round(m, c - 2, r)
                    if "P" in has and 5 <= r < 5 + K:
                        table_step(p, c, r - 5)
                    if "P" in has and r == 5 + K:
                        upper_parts(p, c)
                    if "Z" in has and r == 8:
                        norm_inverse(n, c - 3)
                    if at(s, 2) and r % 2 == 0 and 2 <= r:
                        degree_chunk(r // 2)
                        if r // 2 == 6:
                            degree_chunk(7)
                            degree_small(H * CH, H * B)
                    if at(s, 3) and r == 4:
                        inverse_logs(H * CH, H * B, 1)
                if "M" in has:
                    fold(m, c - 2)

            setup_weights()
            steps(dve, one_step)

        @block.gpsimd
        def _(pool):
            fills = [(w_pq[D:D + 1, D:2 * D], 0.0), (eps_col[:], EPS),
                     (table[0][:, :, 0:1], EMPTY), (table[1][:, :, 0:1], EMPTY)]
            for i in range(4):
                fills += [(xT[i][0:D, :, P:PAD], 0.0), (xT[i][D:D + 1], 1.0)]
            for i, (dst, value) in enumerate(fills):
                wait(pool, s_fill, i)
                nc.gpsimd.memset(dst, value).then_inc(s_fill, 1)
            pool.wait_ge(s_fill, len(fills))
            pool.wait_ge(s_const, 16 * CONST_LOADS)
            nc.gpsimd.tensor_scalar(w_qq[:, D:2 * D], w_qq[:, 0:D], -1.0, None, ALU.mult).then_inc(s_fill, 1)
            assert len(fills) + 1 == FILLED

            def neighbours(b, c):
                wait(pool, s_adjT, b + 1)
                wait(pool, s_hot_ps, FILLS * (b - 1))
                pool.sem_inc(s_go_mask, 1)
                nc.gpsimd.tensor_scalar(mask[c % 2][:], adjT[c % 2][:], 0.0, None, ALU.is_gt).then_inc(s_mask, 1)

            def statistics(b, c):
                wait(pool, s_uv, b + 1)
                wait(pool, s_msT_ps, b - 1)
                wait(pool, s_std, b - 1)
                u, v = uv[c % 2][:, :, 0, :], uv[c % 2][:, :, 1, :]
                p, mean = pq[c % 2][:, :, 0, :], ms[c % 2][:, :, 0, :]
                part = deg_part[:, bass.ds(H * b, H)].unsqueeze(2).to_broadcast([P, H, D])
                tensors = ((pool_a[:], p, part, ALU.mult), (mean, pool_a[:], u, ALU.add),
                           (pool_a[:], p, pool_a[:], ALU.subtract), (pool_b[:], mean, u, ALU.add),
                           (pool_b[:], pool_a[:], pool_b[:], ALU.mult), (pool_c[:], u, u, ALU.mult),
                           (pool_c[:], v, pool_c[:], ALU.subtract), (pool_c[:], pool_c[:], pool_b[:], ALU.add))
                for i, (dst, a, b_, op) in enumerate(tensors):
                    wait(pool, s_stat, STATS * b + i)
                    nc.gpsimd.tensor_tensor(dst, a, b_, op).then_inc(s_stat, 1)
                wait(pool, s_stat, STATS * b + len(tensors))
                pool.sem_inc(s_go_var, 1)
                nc.gpsimd.tensor_scalar(var[c % 2][:], pool_c[:], 0.0, None, ALU.max).then_inc(s_stat, 1)

            def lower_parts(b, c):
                wait(pool, s_upper, b + 1)
                wait(pool, s_tabT_ps, TFILLS * (b - 1))
                nc.gpsimd.tensor_tensor(parts[c % 2][:, :, 1, :], table[c % 2][:], parts[c % 2][:, :, 0, :], ALU.subtract) \
                    .then_inc(s_lower, 1)

            def scaled_sum(b, c):
                wait(pool, s_z, b + 1)
                wait(pool, s_y, 3 * b)
                scale = scaler[:, bass.ds(H * b, H), :].unsqueeze(3).to_broadcast([P, H, 2, D])
                nc.gpsimd.tensor_tensor(zs[:], z[c % 2][:, :, 1:3, :], scale, ALU.mult).then_inc(s_y, 1)
                wait(pool, s_y, 3 * b + 1)
                nc.gpsimd.tensor_tensor(y1[:], z[c % 2][:, :, 0, :], zs[:, :, 0, :], ALU.add).then_inc(s_y, 1)
                wait(pool, s_y, 3 * b + 2)
                wait(pool, s_res, b - 1)
                nc.gpsimd.tensor_tensor(y[c % 2][:], y1[:], zs[:, :, 1, :], ALU.add).then_inc(s_y, 1)

            def normalise(b, c):
                wait(pool, s_rstd, b + 1)
                wait(pool, s_out[c % 2], half(b, c) - 16)
                nc.gpsimd.tensor_tensor(result[c % 2][:], y[c % 2][:], rstd[:, c % 2, :].unsqueeze(2).to_broadcast([P, H, D]),
                                        ALU.mult).then_inc(s_res, 1)

            def one_step(s, c, has):
                if "Q" in has:
                    if at(s, 1):
                        pool.wait_ge(s_deg, DEG_FIRST)
                    if at(s, 3):
                        pool.wait_ge(s_deg, DEG_ALL)
                    statistics(s - 1, c - 1)
                if "P" in has:
                    neighbours(s, c)
                if "Z" in has:
                    if at(s, 3):
                        pool.wait_ge(s_log, 6)
                    scaled_sum(s - 3, c - 3)
                    normalise(s - 3, c - 3)
                if "P" in has:
                    lower_parts(s, c)

            steps(pool, one_step)


_INS = ["x", "adj", "L0_gnn_W_pre", "L0_gnn_b_pre", "L0_gnn_W_post", "L0_gnn_b_post"]


def kernel(**inputs):
    import numpy as _np
    import concourse.bacc as _bacc
    from concourse import mybir as _mybir
    from concourse.bass_utils import run_bass_kernel_spmd as _run

    nc = _bacc.Bacc("TRN2", target_bir_lowering=False, num_devices=1)
    arrays, args = {}, []
    given = [(name, inputs[name]) for name in _INS] + list(zip(("ident", "sign", "bias"), constants()))
    for name, a in given:
        a = _np.ascontiguousarray(a)
        arrays[f"in_{name}_dram"] = a
        args.append(nc.dram_tensor(f"in_{name}_dram", a.shape, _mybir.dt.from_np(a.dtype), kind="ExternalInput").ap())
    args.append(nc.dram_tensor("out_0_dram", (B, N, D), F32, kind="ExternalOutput").ap())
    pna_layer(nc, *args)
    r = _run(nc, [arrays], core_ids=[0])
    return r.results[0]["out_0_dram"]
```

```python
from contextlib import ExitStack

import numpy as np

import concourse.bass as bass
from concourse import mybir

F32 = mybir.dt.float32
F32R = mybir.dt.float32r
BF16 = mybir.dt.bfloat16
ALU = mybir.AluOpType
ACT = mybir.ActivationFunctionType
AX = mybir.AxisListType

P = 128
B, N, D = 32, 256, 64
H = N // P
K = 5
S = 2 ** K
ROWS = 2 * S
TILES = P // ROWS
GH = -(-P // K)
G = H * GH
R = G // TILES
PAD = GH * K
RH = R // H
FILLS = R // 2
TFILLS = -(-R // 4)
J = 3
AVG_D_LOG = 4.86
EPS = 1e-05
EMPTY = -1e9
CH = 4
CHUNKS = B // CH
TAB = K - 1 + H
STATS = 9
T_SLOTS = (4, 6, 7, 8, 9, 10, 11)
TAB_SLOTS = (6, 7, 8, 9, 10, 11)
STORE_LAG = 6
DEG_SMALL = 4
DVE_CHUNKS = 4
TREE_FIRST = 2
TREE = 8
assert 2 ** TREE == N
LOOP_FIRST, UNROLL = 8, 4
LOOP_TRIPS = (B - LOOP_FIRST) // UNROLL


def constants():
    sign = np.zeros((P, RH, TILES, 2, S), np.float32)
    for g in range(GH):
        for i in range(min(K, P - K * g)):
            for s in range(S):
                sign[K * g + i, g // TILES, g % TILES, :, s] = 1.0 if s >> i & 1 else -1.0
    bias = np.array([[1.0 - bin(s % S).count("1")] for s in range(P)], np.float32)
    return np.eye(P, dtype=np.float32), sign.reshape(P, -1), bias


def pna_layer(nc, x, adj, w_pre, b_pre, w_post, b_post, ident_in, sign_in, bias_in, out):
    with ExitStack() as ctx:
        def sb(name, shape, dt=F32):
            return ctx.enter_context(nc.sbuf_tensor(name, shape, dt))

        def sem(name):
            return ctx.enter_context(nc.semaphore(name))

        ident = sb("ident", [P, P])
        ident_r = sb("ident_r", [P, P], F32R)
        sign_f = sb("sign_f", [P, RH, P])
        sign = sb("sign", [P, RH, P], BF16)
        hot_bias = sb("hot_bias", [P, 1])
        w_pq = sb("w_pq", [D + 1, 2 * D])
        w_qq = sb("w_qq", [D, 2 * D])
        w_pT = sb("w_pT", [D, D + 1])
        w_fold = sb("w_fold", [D, 2, J, D])
        w_sum = sb("w_sum", [D, J, D])
        w_x = sb("w_x", [D + 1, J, D])
        w_x0 = sb("w_x0", [D + 1, D])
        w_ms = sb("w_ms", [P, J, D])
        w_mx = sb("w_mx", [P, J, D])
        w_mean = sb("w_mean", [P, 3, J])
        adj_all = sb("adj_all", [P, 2, CH, H, N])
        deg = sb("deg", [P, B * H])
        deg1 = sb("deg1", [P, B * H])
        deg_safe = sb("deg_safe", [P, B * H])
        deg_inv = sb("deg_inv", [P, B * H])
        deg_part = sb("deg_part", [P, B * H])
        scaler = sb("scaler", [P, B * H, 2])
        x_in = [sb(f"x_in{i}", [P, H, D]) for i in range(2)]
        adj_in = [sb(f"adj_in{i}", [P, H, N]) for i in range(2)]
        adjT = [sb(f"adjT{i}", [P, H, N]) for i in range(2)]
        mask = [sb(f"mask{i}", [P, H, N], BF16) for i in range(2)]
        xT = [sb(f"xT{i}", [D + 1, H, PAD]) for i in range(4)]
        pq = [sb(f"pq{i}", [P, H, 3, D]) for i in range(2)]
        table = [sb(f"table{i}", [P, G, S]) for i in range(2)]
        parts = [sb(f"parts{i}", [P, G, 2, S], F32R) for i in range(2)]
        tableT = [sb(f"tableT{i}", [P, R, P], F32R) for i in range(2)]
        hot = [sb(f"hot{i}", [P, R, N], F32R) for i in range(2)]
        acc = [sb(f"acc{i}", [P, 2, 2, N]) for i in range(2)]
        folded = sb("folded", [P, 2, N])
        best = [sb(f"best{i}", [P, N]) for i in range(2)]
        uv = [sb(f"uv{i}", [P, H, 2, D]) for i in range(2)]
        pool_a = sb("pool_a", [P, H, D])
        pool_b = sb("pool_b", [P, H, D])
        pool_c = sb("pool_c", [P, H, D])
        var = [sb(f"var{i}", [P, H, D]) for i in range(2)]
        ms = [sb(f"ms{i}", [P, H, 2, D]) for i in range(2)]
        msT = [sb(f"msT{i}", [P, H, P]) for i in range(4)]
        z = [sb(f"z{i}", [P, H, J, D]) for i in range(2)]
        zs = sb("zs", [P, H, 2, D])
        y1 = sb("y1", [P, H, D])
        y = [sb(f"y_out{i}", [P, H, D]) for i in range(2)]
        y_sq = sb("y_sq", [P, H, D])
        sumsq = sb("sumsq", [P, 2, H])
        root = sb("root", [P, 2, H])
        rstd = sb("rstd", [P, 2, H])
        result = [sb(f"result{i}", [P, H, D]) for i in range(2)]
        eps_col = sb("eps_col", [P, 1])

        ps_main = [ctx.enter_context(nc.psum_tensor(f"ps_main{i}", [P, 2, 2, N], F32)) for i in range(2)]
        ps_hot = [ctx.enter_context(nc.psum_tensor(f"ps_hot{i}", [P, 2, N], F32)) for i in range(2)]
        ps_fold = (ps_main[0][0:D, 0, 0, 0:D + 1], ps_main[1][0:D + 1, 0, 0, 0:J * D])
        ps_a = ctx.enter_context(nc.psum_tensor("ps_a", [P, 4 * P], F32))
        ps_b = ctx.enter_context(nc.psum_tensor("ps_b", [P, 4 * P], F32))

        s_const = sem("early_constants_loaded")
        s_const_late = sem("late_constants_loaded")
        s_x = [sem(f"x_loaded{i}") for i in range(2)]
        s_adj = [sem(f"adj_loaded{i}") for i in range(2)]
        s_all = [sem(f"adj_chunk_loaded{i}") for i in range(2)]
        s_out = [sem(f"stored{i}") for i in range(2)]
        s_fill = sem("fills_done")
        s_setup = sem("setup_step")
        s_setup_pe = sem("setup_pe")
        s_signs = sem("constants_ready")
        s_deg = sem("deg_step")
        s_tree = sem("deg_tree_step")
        s_sign_in = sem("sign_loaded")
        s_log = sem("log_ready")
        s_adjT_ps = sem("adjT_in_psum")
        s_xT_ps = sem("xT_in_psum")
        s_q_ps = sem("q_in_psum")
        s_pq_ps = sem("pq_in_psum")
        s_tabT_ps = sem("tableT_in_psum")
        s_hot_ps = sem("hot_in_psum")
        s_sum_ps = sem("sums_in_psum")
        s_msT_ps = sem("msT_in_psum")
        s_z_ps = sem("z_in_psum")
        s_round = sem("round_in_psum")
        s_adjT = sem("adjT_ready")
        s_xT = sem("xT_ready")
        s_p = sem("p_ready")
        s_pq = sem("pq_ready")
        s_tabT = sem("tableT_ready")
        s_hot = sem("hot_ready")
        s_uv = sem("uv_ready")
        s_std = sem("std_ready")
        s_msT = sem("msT_ready")
        s_acc0 = sem("acc_started")
        s_z = sem("z_copied")
        s_sq = sem("sumsq_ready")
        s_root = sem("root_ready")
        s_tab = sem("table_step")
        s_upper = sem("upper_parts_ready")
        s_acc = sem("acc_step")
        s_fold = sem("fold_step")
        s_rstd = sem("rstd_ready")
        s_go_x = sem("go_x_transposes")
        s_go_mask = sem("go_mask")
        s_go_var = sem("go_var")
        s_mask = sem("mask_ready")
        s_lower = sem("lower_parts_ready")
        s_stat = sem("stats_step")
        s_y = sem("y_step")
        s_res = sem("result_ready")

        def wait(eng, s, value):
            if not isinstance(value, int) or value > 0:
                eng.wait_ge(s, value)

        def half(b, c):
            return 8 * b + (16 - 8 * (c % 2))

        def at(s, n):
            return isinstance(s, int) and s == n

        def steps(eng, one_step):
            def has(s):
                return "".join(n for i, n in enumerate("PQMZ") if 0 <= s - i < B)
            for s in range(LOOP_FIRST):
                one_step(s, s % 4, has(s))
            with eng.Fori(0, LOOP_TRIPS) as i:
                for u in range(UNROLL):
                    one_step(UNROLL * i + (LOOP_FIRST + u), u, "PQMZ")
            for s in range(B, B + 3):
                one_step(s, s % 4, has(s))

        x_rows = x.rearrange("b (p t) d -> b p t d", t=H)
        adj_rows = adj.rearrange("b (p t) m -> b p t m", t=H)
        out_rows = out.rearrange("b (p t) d -> b p t d", t=H)
        post = w_post[D:, :].rearrange("(j k d) o -> k d j o", j=J, k=4)
        EARLY, LATE = 6, 8
        FILLED = 13
        SET_UP = 21

        DEG_FIRST = 1 + DEG_SMALL
        DEG_SECOND = DVE_CHUNKS + 2 * DEG_SMALL
        DEG_ALL = DEG_SECOND + DEG_SMALL

        block = ctx.enter_context(nc.Block())

        @block.sync
        def _(sp):
            def load(b, c):
                wait(sp, s_adjT_ps, b - 1)
                sp.dma_start(adj_in[c % 2][:], adj_rows[b]).then_inc(s_adj[c % 2], 16)
                wait(sp, s_xT_ps, b - 1)
                sp.dma_start(x_in[c % 2][:], x_rows[b]).then_inc(s_x[c % 2], 16)

            early = [
                (ident[:], ident_in),
                (w_qq[:, 0:D], w_pre[D:2 * D, :]), (w_pq[0:D, 0:D], w_pre[0:D, :]),
                (w_pq[0:D, D:2 * D], w_pre[D:2 * D, :]), (w_pq[D:D + 1, 0:D], b_pre.rearrange("(a d) -> a d", a=1)),
                (hot_bias[:], bias_in),
            ]
            late = [
                (w_x0[0:D, :], w_post[0:D, :]), (w_x0[D:D + 1, :], b_post.rearrange("(a d) -> a d", a=1)),
                (w_ms[0:D, :, :], post[0]), (w_ms[D:2 * D, :, :], post[3]),
                (w_mx[0:D, :, :], post[1]), (w_mx[D:2 * D, :, :], post[2]),
                (w_fold[:, 0, :, :], post[1]), (w_fold[:, 1, :, :], post[2]),
            ]
            assert (len(early), len(late)) == (EARLY, LATE)

            def load_chunk(c):
                if c >= 2:
                    if c - 2 < DVE_CHUNKS:
                        sp.wait_ge(s_deg, 1 if c == 2 else 1 + DEG_SMALL + c - 2)
                    else:
                        sp.wait_ge(s_tree, TREE * (c - 1 - DVE_CHUNKS))
                sp.dma_start(adj_all[:, c % 2], adj_rows[CH * c:CH * c + CH].rearrange("b p t m -> p b t m")) \
                    .then_inc(s_all[c % 2], 16)

            sp.dma_start(*early[0]).then_inc(s_const, 16)
            load(0, 0)
            for dst, src in early[1:]:
                sp.dma_start(dst, src).then_inc(s_const, 16)
            sp.dma_start(sign_f[:].rearrange("p r c -> p (r c)"), sign_in).then_inc(s_sign_in, 16)
            load_chunk(0)
            load(1, 1)
            for dst, src in late:
                sp.dma_start(dst, src).then_inc(s_const_late, 16)
            def store(b, c):
                wait(sp, s_res, b + 1)
                sp.dma_start(out_rows[b], result[c % 2][:]).then_inc(s_out[c % 2], 16)

            load_chunk(1)
            for b in range(2, 2 * UNROLL):
                load_chunk(b)
                load(b, b % 4)
                if b >= STORE_LAG:
                    store(b - STORE_LAG, (b - STORE_LAG) % 4)
            with sp.Fori(0, B // UNROLL - 2) as i:
                for u in range(UNROLL):
                    load(UNROLL * i + (2 * UNROLL + u), u)
                    store(UNROLL * i + (2 * UNROLL + u - STORE_LAG), (u - STORE_LAG) % 4)
            for b in range(B - STORE_LAG, B):
                store(b, b % 4)
            for c in range(2):
                sp.wait_ge(s_out[c], 16 * B // 2)

        @block.tensor
        def _(pe):
            def transpose_p():
                pe.transpose(ps_fold[0], w_pq[:, 0:D], ident[0:D + 1, 0:D + 1]).then_inc(s_setup_pe, 1)

            def fold_p():
                pe.wait_ge(s_setup, 2)
                pe.matmul(ps_fold[1], w_pT[:], w_sum[:].rearrange("d j o -> d (j o)"), start=True, stop=True) \
                    .then_inc(s_setup_pe, 1)

            def adj_transposes(b, c):
                wait(pe, s_adj[c % 2], half(b, c))
                wait(pe, s_pq, b)
                wait(pe, s_tabT, TFILLS * (b - 1))
                for k in range(H):
                    for t in range(H):
                        last = pe.transpose(ps_a[:, (k * H + t) * P:(k * H + t + 1) * P],
                                            adj_in[c % 2][:, t, k::H], ident[:])
                last.then_inc(s_adjT_ps, 1)

            def x_transposes(b, c):
                wait(pe, s_x[c % 2], half(b, c))
                wait(pe, s_adjT, b + 1)
                pe.sem_inc(s_go_x, 1)
                for t in range(H):
                    last = pe.transpose(ps_a[0:D, t * P:(t + 1) * P], x_in[c % 2][:, t, :], ident[:])
                last.then_inc(s_xT_ps, 1)

            def q_rows(b, c):
                wait(pe, s_xT, b + 1)
                wait(pe, s_uv, b)
                wait(pe, s_z, b - 2)
                pe.matmul(ps_b[:, 0:H * PAD], w_qq[:], xT[c % 4][0:D].rearrange("d t m -> d (t m)"),
                          start=True, stop=True).then_inc(s_q_ps, 1)

            def pq_nodes(b, c):
                wait(pe, s_xT, b + 1)
                wait(pe, s_tabT, TFILLS * (b - 1) + 1)
                for t in range(H):
                    last = pe.matmul(ps_a[:, t * P:(t + 1) * P], xT[c % 4][:, t, 0:P], w_pq[:], start=True, stop=True)
                last.then_inc(s_pq_ps, 1)

            def hot_rows(b, c, f):
                wait(pe, s_hot, FILLS * b + f - 1)
                for r in range(2 * f, 2 * f + 2):
                    last = pe.matmul(ps_hot[(c + f) % 2][:, r % 2, :], sign[:, r % RH, :], mask[c % 2][:, r // RH, :],
                                     start=True, stop=True)
                last.then_inc(s_hot_ps, 1)

            def table_transposes(b, c, f, has):
                wait(pe, s_lower, H * b + (1 if 4 * (f + 1) <= RH else H))
                if "P" in has:
                    if f == 0:
                        wait(pe, s_xT, b + 2)
                    elif f == 1:
                        wait(pe, s_pq, b + 2)
                wait(pe, s_tabT, TFILLS * b + f)
                for r in range(4 * f, min(4 * f + 4, R)):
                    last = pe.transpose(ps_a[:, (r % 4) * P:(r % 4 + 1) * P].bitcast(F32R),
                                        parts[c % 2][:, TILES * r:TILES * r + TILES].rearrange("p g a s -> p (g a s)"),
                                        ident_r[:])
                last.then_inc(s_tabT_ps, 1)

            def neighbour_sums(b, c):
                wait(pe, s_adjT, b + 1)
                wait(pe, s_pq, b + 1)
                wait(pe, s_tab, TAB * (b + 1))
                wait(pe, s_msT, b)
                for t in range(H):
                    for k in range(H):
                        last = pe.matmul(ps_b[:, t * P:(t + 1) * P], adjT[c % 2][:, k, t * P:(t + 1) * P],
                                         pq[c % 2][:, k, 1:3, :].rearrange("p a d -> p (a d)"),
                                         start=(k == 0), stop=(k == H - 1))
                last.then_inc(s_sum_ps, 1)

            def look_up(b, c, f):
                if f == 2:
                    wait(pe, s_acc0, b + 1)
                elif f > 2:
                    wait(pe, s_acc, (FILLS - 1) * b + f - 2)
                else:
                    wait(pe, s_acc, (FILLS - 1) * (b - 1) + FILLS - 2 + f)
                wait(pe, s_hot, FILLS * b + f + 1)
                if f % 2 == 0:
                    wait(pe, s_tabT, TFILLS * b + f // 2 + 1)
                for r in range(2 * f, 2 * f + 2):
                    for j in range(TILES):
                        rows = slice(ROWS * j, ROWS * (j + 1))
                        last = pe.matmul(ps_main[(c + f) % 2][:, j, r % 2, :], tableT[c % 2][rows, r, :],
                                         hot[c % 2][rows, r, :], start=True, stop=True)
                last.then_inc(s_round, 1)

            def ms_transposes(b, c, has):
                wait(pe, s_std, b + 1)
                if "Q" in has:
                    wait(pe, s_tab, TAB * (b + 2))
                wait(pe, s_z, b - 1)
                for t in range(H):
                    last = pe.transpose(ps_b[:, t * P:(t + 1) * P], ms[c % 2][:, t].rearrange("p a d -> p (a d)"), ident[:])
                last.then_inc(s_msT_ps, 1)

            def z_nodes(b, c, t, has):
                if t == 0:
                    wait(pe, s_z, b)
                    wait(pe, s_msT, min(b + 2, B) if isinstance(b, int) else b + 2)
                    if "Q" in has:
                        wait(pe, s_uv, b + 3)
                zt = ps_b[:, t * J * D:(t + 1) * J * D]
                pe.matmul(zt, xT[c % 4][:, t, 0:P], w_x[:].rearrange("d j o -> d (j o)"), start=True, stop=False)
                pe.matmul(zt, msT[c % 4][:, t, :], w_ms[:].rearrange("d j o -> d (j o)"), start=False, stop=False)
                if t == 0:
                    wait(pe, s_fold, 2 * (b + 1))
                last = pe.matmul(zt, best[c % 2][:, t * P:(t + 1) * P], w_mx[:].rearrange("d j o -> d (j o)"),
                                 start=False, stop=True)
                if t == H - 1:
                    last.then_inc(s_z_ps, 1)

            def one_step(s, c, has):
                p, q, m, n = s, s - 1, s - 2, s - 3
                if at(s, 1):
                    pe.wait_ge(s_signs, 3)
                if at(s, 2):
                    pe.wait_ge(s_setup, 3)
                if at(s, 3):
                    pe.wait_ge(s_setup, SET_UP)
                for f in range(FILLS):
                    if "M" in has:
                        look_up(m, c - 2, f)
                    if "M" in has and f == 0:
                        ms_transposes(m, c - 2, has)
                    if "P" in has and f == 6:
                        q_rows(p, c)
                    if "Q" in has and f in T_SLOTS:
                        table_transposes(q, c - 1, T_SLOTS.index(f), has)
                    if "Q" in has and f == 0:
                        wait(pe, s_mask, s)
                    if "Q" in has:
                        hot_rows(q, c - 1, f)
                    if "Q" in has and f == 1:
                        neighbour_sums(q, c - 1)
                    if "P" in has and f == 0:
                        adj_transposes(p, c)
                    if "P" in has and f == 2:
                        x_transposes(p, c)
                    if "P" in has and f == 5:
                        pq_nodes(p, c)
                    if "Z" in has and f in (3, 4):
                        z_nodes(n, c - 3, f - 3, has)
                    if at(s, 1) and f == 2:
                        fold_p()
                if at(s, 0):
                    transpose_p()

            pe.wait_ge(s_const, 16 * EARLY)
            pe.wait_ge(s_fill, FILLED)
            steps(pe, one_step)

        @block.scalar
        def _(act):
            def adjT_copy(b, c):
                wait(act, s_adjT_ps, b + 1)
                wait(act, s_sum_ps, b - 1)
                wait(act, s_mask, b - 1)
                nc.scalar.activation(adjT[c % 2][:].rearrange("p k n -> p (k n)"), ps_a[:], ACT.Copy).then_inc(s_adjT, 1)

            def xT_copy(b, c):
                wait(act, s_xT_ps, b + 1)
                wait(act, s_z_ps, b - 3)
                nc.scalar.activation(xT[c % 4][0:D, :, 0:P], ps_a[0:D, 0:H * P].rearrange("p (t m) -> p t m", t=H),
                                     ACT.Copy).then_inc(s_xT, 1)

            def pq_copy(b, c):
                wait(act, s_pq_ps, b + 1)
                wait(act, s_sum_ps, b - 1)
                wait(act, s_stat, STATS * (b - 1))
                src = ps_a[:, 0:H * P].rearrange("p (t a d) -> p t a d", t=H, a=2)
                nc.scalar.activation(pq[c % 2][:, :, 0:2, :], src, ACT.Copy).then_inc(s_p, 1)
                nc.scalar.activation(pq[c % 2][:, :, 2, :], src[:, :, 1, :], ACT.Square).then_inc(s_pq, 1)

            def hot_copy(b, c, f):
                wait(act, s_hot_ps, FILLS * b + f + 1)
                if f == 0:
                    wait(act, s_round, FILLS * (b - 1))
                nc.scalar.activation(hot[c % 2][:, 2 * f:2 * f + 2, :], ps_hot[(c + f) % 2][:], ACT.Relu,
                                     bias=hot_bias[:, 0:1]).then_inc(s_hot, 1)

            def tableT_copy(b, c, f):
                wait(act, s_tabT_ps, TFILLS * b + f + 1)
                n = min(4, R - 4 * f)
                nc.scalar.activation(tableT[c % 2][:, 4 * f:4 * f + n, :],
                                     ps_a[:, 0:n * P].rearrange("p (r m) -> p r m", m=P), ACT.Copy).then_inc(s_tabT, 1)

            def uv_copy(b, c):
                wait(act, s_sum_ps, b + 1)
                wait(act, s_stat, STATS * (b - 1))
                for t in range(H):
                    last = nc.scalar.activation(uv[c % 2][:, t].rearrange("p a d -> p (a d)"), ps_b[:, t * P:(t + 1) * P],
                                                ACT.Copy, scale=deg_inv[:, bass.ds(H * b + t, 1)])
                last.then_inc(s_uv, 1)

            def std_root(b, c):
                wait(act, s_stat, STATS * (b + 1))
                nc.scalar.activation(ms[c % 2][:, :, 1, :], var[c % 2][:], ACT.Sqrt, bias=eps_col[:, 0:1]) \
                    .then_inc(s_std, 1)

            def msT_copy(b, c):
                wait(act, s_msT_ps, b + 1)
                wait(act, s_z_ps, b - 3)
                nc.scalar.activation(msT[c % 4][:].rearrange("p t n -> p (t n)"), ps_b[:, 0:H * P], ACT.Copy) \
                    .then_inc(s_msT, 1)

            def upper_parts(b, c, k):
                wait(act, s_tab, TAB * b + K + k)
                wait(act, s_tabT_ps, TFILLS * (b - 1))
                g = slice(GH * k, GH * (k + 1))
                nc.scalar.activation(parts[c % 2][:, g, 0, :], table[c % 2][:, g, :], ACT.Copy) \
                    .then_inc(s_upper, 1)

            def start_acc(b, c):
                wait(act, s_round, FILLS * b + 1)
                wait(act, s_fold, 2 * (b - 1))
                nc.scalar.activation(acc[c % 2][:], ps_main[c % 2][:], ACT.Copy).then_inc(s_acc0, 1)

            def z_copy(b, c):
                wait(act, s_z_ps, b + 1)
                wait(act, s_y, 3 * (b - 1))
                nc.scalar.activation(z[c % 2][:].rearrange("p t j o -> p (t j o)"), ps_b[:, 0:H * J * D], ACT.Copy) \
                    .then_inc(s_z, 1)

            def square_sums(b, c):
                wait(act, s_y, 3 * (b + 1))
                wait(act, s_root, b - 1)
                for t in range(H):
                    nc.scalar.activation(y_sq[:, t, :], y[c % 2][:, t, :], ACT.Square, accum_out=sumsq[:, c % 2, t:t + 1]) \
                        .then_inc(s_sq, 1)

            def norm_root(b, c):
                wait(act, s_sq, H * (b + 1))
                if at(b, 0):
                    act.wait_ge(s_signs, 1)
                wait(act, s_rstd, b - 1)
                nc.scalar.activation(root[:, c % 2, :], sumsq[:, c % 2, :], ACT.Sqrt, bias=eps_col[:, 0:1],
                                     scale=1.0 / D).then_inc(s_root, 1)

            def set_up():
                nc.scalar.activation(root[:, 0, 0:1], eps_col[:], ACT.Sqrt).then_inc(s_signs, 1)
                act.wait_ge(s_const, 16 * EARLY)
                nc.scalar.activation(ident_r[:], ident[:], ACT.Copy).then_inc(s_signs, 1)

            def convert_signs():
                act.wait_ge(s_sign_in, 16)
                nc.scalar.activation(sign[:], sign_f[:], ACT.Copy).then_inc(s_signs, 1)

            def logs(a, b, degrees):
                wait(act, s_deg, degrees)
                nc.scalar.activation(scaler[:, a:b, 0], deg1[:, a:b], ACT.Ln).then_inc(s_log, 1)

            def one_step(s, c, has):
                p, q, m, n = s, s - 1, s - 2, s - 3
                if at(s, 0):
                    set_up()
                if at(s, 1):
                    upper_parts(0, 0, 1)
                if at(s, 3):
                    logs(0, H * CH * DVE_CHUNKS, DEG_SECOND)
                if at(s, 7):
                    logs(H * CH * DVE_CHUNKS, H * B, DEG_ALL)
                for f in range(FILLS):
                    if "M" in has and f == 0:
                        start_acc(m, c - 2)
                        msT_copy(m, c - 2)
                    if "P" in has and f == 0:
                        adjT_copy(p, c)
                    if "Q" in has and f == 0 and not at(s, 1):
                        upper_parts(q, c - 1, 1)
                    if "Q" in has and f == 1:
                        if at(s, 1):
                            act.wait_ge(s_deg, DEG_FIRST)
                        if at(s, 5):
                            act.wait_ge(s_deg, DEG_SECOND)
                        uv_copy(q, c - 1)
                    if "P" in has and f == 12:
                        upper_parts(p, c, 0)
                    if "Q" in has and f in T_SLOTS:
                        tableT_copy(q, c - 1, T_SLOTS.index(f))
                    if "Q" in has:
                        hot_copy(q, c - 1, f)
                    if "P" in has and f == 2:
                        xT_copy(p, c)
                    if "Z" in has and f == 4:
                        z_copy(n, c - 3)
                    if "P" in has and f == 5:
                        pq_copy(p, c)
                        if at(s, 0):
                            convert_signs()
                    if "Z" in has and f == 8:
                        square_sums(n, c - 3)
                    if "Q" in has and f == 8:
                        std_root(q, c - 1)
                    if "Z" in has and f == 9:
                        norm_root(n, c - 3)

            act.wait_ge(s_fill, FILLED - 1)
            steps(act, one_step)

        @block.vector
        def _(dve):
            def table_step(b, c, i):
                if i == 0:
                    wait(dve, s_q_ps, b + 1)
                    wait(dve, s_lower, H * (b - 1))
                if i < K:
                    wait(dve, s_tab, TAB * b + i)
                g = slice(0, G) if i < K - 1 else slice(GH * (i - K + 1), GH * (i - K + 2))
                i = min(i, K - 1)
                node = ps_b[:, 0:H * PAD].rearrange("p (g i) -> p g i", i=K)[:, g, i:i + 1].to_broadcast([P, g.stop - g.start, 1 << i])
                nc.vector.tensor_tensor(table[c % 2][:, g, 1 << i:2 << i], table[c % 2][:, g, 0:1 << i], node, ALU.max) \
                    .then_inc(s_tab, 1)

            def take_round(b, c, r):
                wait(dve, s_round, FILLS * b + r + 1)
                if r == 1:
                    wait(dve, s_acc0, b + 1)
                else:
                    wait(dve, s_acc, (FILLS - 1) * b + r - 1)
                a = acc[c % 2][:]
                nc.vector.tensor_tensor(a, ps_main[(c + r) % 2][:], a, ALU.max).then_inc(s_acc, 1)

            def fold(b, c, part):
                a = acc[c % 2]
                if part == 0:
                    wait(dve, s_acc, (FILLS - 1) * (b + 1))
                    wait(dve, s_fold, 2 * b)
                    nc.vector.tensor_tensor(folded[:], a[:, 0], a[:, 1], ALU.max).then_inc(s_fold, 1)
                else:
                    wait(dve, s_z_ps, b - 1)
                    wait(dve, s_fold, 2 * b + 1)
                    nc.vector.tensor_tensor(best[c % 2][:], folded[:, 0, :], folded[:, 1, :], ALU.max).then_inc(s_fold, 1)

            def norm_inverse(b, c):
                wait(dve, s_root, b + 1)
                wait(dve, s_res, b - 1)
                nc.vector.reciprocal(rstd[:, c % 2, :], root[:, c % 2, :]).then_inc(s_rstd, 1)

            done = [0]

            def degree_chunk(c):
                wait(dve, s_all[c % 2], 16 * (c // 2 + 1))
                nc.vector.tensor_reduce(deg[:, H * CH * c:H * CH * (c + 1)], adj_all[:, c % 2].rearrange("p b t m -> p (b t) m"),
                                        AX.X, ALU.add).then_inc(s_deg, 1)
                done[0] += 1

            def degree_small(a, b):
                for out_, op in ((deg1, lambda: nc.vector.tensor_scalar(deg1[:, a:b], deg[:, a:b], 1.0, None, ALU.add)),
                                 (deg_safe, lambda: nc.vector.tensor_scalar(deg_safe[:, a:b], deg[:, a:b], 1.0, None, ALU.max)),
                                 (deg_inv, lambda: nc.vector.reciprocal(deg_inv[:, a:b], deg_safe[:, a:b])),
                                 (deg_part, lambda: nc.vector.tensor_tensor(deg_part[:, a:b], deg[:, a:b], deg_inv[:, a:b],
                                                                            ALU.mult))):
                    dve.wait_ge(s_deg, done[0])
                    op().then_inc(s_deg, 1)
                    done[0] += 1

            def inverse_logs(a, b, logged):
                dve.wait_ge(s_log, logged)
                nc.vector.tensor_scalar(scaler[:, a:b, 1], scaler[:, a:b, 0], EPS, None, ALU.max).then_inc(s_log, 1)
                dve.wait_ge(s_log, logged + 1)
                nc.vector.reciprocal(scaler[:, a:b, 1], scaler[:, a:b, 1]).then_inc(s_log, 1)

            setups = [0]

            def link(ins, behind=0):
                setups[0] += 1
                ins.then_inc(s_setup, 1)
                dve.wait_ge(s_setup, setups[0] - behind)

            def setup_weights():
                dve.wait_ge(s_const_late, 16 * LATE)
                dve.wait_ge(s_setup_pe, 1)
                link(nc.vector.tensor_copy(w_pT[:], ps_fold[0]))
                link(nc.vector.tensor_tensor(w_sum[:], w_fold[:, 0], w_fold[:, 1], ALU.add))

            def finish_weights():
                dve.wait_ge(s_setup_pe, 2)
                link(nc.vector.tensor_copy(w_x[:], ps_fold[1].rearrange("d (j o) -> d j o", j=J)))
                link(nc.vector.tensor_tensor(w_x0[0:D, :], w_x0[0:D, :], ident[0:D, 0:D], ALU.add))
                link(nc.vector.tensor_tensor(w_x[:, 0, :], w_x[:, 0, :], w_x0[:], ALU.add))
                link(nc.vector.tensor_scalar(w_mx[D:2 * D], w_mx[D:2 * D], -1.0, None, ALU.mult))
                weights = [(i, w, w.shape[0]) for i, w in enumerate((w_x, w_ms, w_mx))]
                for i, w, k in weights:
                    link(nc.vector.tensor_scalar(w[:, 1, :], w[:, 1, :], 1.0 / AVG_D_LOG, None, ALU.mult), 2)
                for i, w, k in weights:
                    link(nc.vector.tensor_scalar(w[:, 2, :], w[:, 2, :], AVG_D_LOG, None, ALU.mult), 2)
                for i, w, k in weights:
                    link(nc.vector.tensor_reduce(w_mean[0:k, i, :], w[:], AX.X, ALU.add), 2)
                for i, w, k in weights:
                    link(nc.vector.tensor_scalar(w_mean[0:k, i, :], w_mean[0:k, i, :], 1.0 / D, None, ALU.mult), 2)
                for i, w, k in weights:
                    link(nc.vector.tensor_tensor(w[:], w[:], w_mean[0:k, i, :].unsqueeze(2).to_broadcast([k, J, D]),
                                                 ALU.subtract), 2)
                dve.wait_ge(s_setup, SET_UP)

            def one_step(s, c, has):
                p, q, m, n = s, s - 1, s - 2, s - 3
                for r in range(FILLS):
                    if "M" in has and r:
                        take_round(m, c - 2, r)
                    if "P" in has and r in TAB_SLOTS:
                        table_step(p, c, TAB_SLOTS.index(r))
                    if "Z" in has and r in (1, 2):
                        fold(n, c - 3, r - 1)
                    if "Z" in has and r == FILLS - 1:
                        norm_inverse(n, c - 3)
                    if at(s, 3) and r == 4:
                        inverse_logs(0, H * CH * DVE_CHUNKS, 1)
                    if at(s, 6) and r == 6:
                        dve.wait_ge(s_tree, TREE * (CHUNKS - DVE_CHUNKS))
                        degree_small(H * CH * DVE_CHUNKS, H * B)
                    if at(s, 7) and r == 4:
                        inverse_logs(H * CH * DVE_CHUNKS, H * B, 4)
                if at(s, 0):
                    degree_chunk(0)
                    degree_small(0, H * CH)
                    setup_weights()
                    degree_chunk(1)
                if at(s, 1):
                    finish_weights()
                    degree_chunk(2)
                    degree_chunk(3)
                    degree_small(H * CH, H * CH * DVE_CHUNKS)
            dve.wait_ge(s_fill, FILLED)
            steps(dve, one_step)

        @block.gpsimd
        def _(pool):
            fills = [(w_pq[D:D + 1, D:2 * D], 0.0), (eps_col[:], EPS),
                     (table[0][:, :, 0:1], EMPTY), (table[1][:, :, 0:1], EMPTY)]
            for i in range(4):
                fills += [(xT[i][0:D, :, P:PAD], 0.0), (xT[i][D:D + 1], 1.0)]
            for i, (dst, value) in enumerate(fills):
                wait(pool, s_fill, i)
                nc.gpsimd.memset(dst, value).then_inc(s_fill, 1)
            pool.wait_ge(s_fill, len(fills))
            pool.wait_ge(s_const, 16 * EARLY)
            nc.gpsimd.tensor_scalar(w_qq[:, D:2 * D], w_qq[:, 0:D], -1.0, None, ALU.mult).then_inc(s_fill, 1)
            assert len(fills) + 1 == FILLED

            def neighbours(b, c):
                wait(pool, s_adjT, b + 1)
                wait(pool, s_hot_ps, FILLS * (b - 1))
                pool.sem_inc(s_go_mask, 1)
                nc.gpsimd.tensor_scalar(mask[c % 2][:], adjT[c % 2][:], 0.0, None, ALU.is_gt).then_inc(s_mask, 1)

            def statistics(b, c):
                wait(pool, s_uv, b + 1)
                wait(pool, s_msT_ps, b - 1)
                wait(pool, s_std, b - 1)
                u, v = uv[c % 2][:, :, 0, :], uv[c % 2][:, :, 1, :]
                p, mean = pq[c % 2][:, :, 0, :], ms[c % 2][:, :, 0, :]
                part = deg_part[:, bass.ds(H * b, H)].unsqueeze(2).to_broadcast([P, H, D])
                tensors = ((pool_a[:], p, part, ALU.mult), (mean, pool_a[:], u, ALU.add),
                           (pool_a[:], p, pool_a[:], ALU.subtract), (pool_b[:], mean, u, ALU.add),
                           (pool_b[:], pool_a[:], pool_b[:], ALU.mult), (pool_c[:], u, u, ALU.mult),
                           (pool_c[:], v, pool_c[:], ALU.subtract), (pool_c[:], pool_c[:], pool_b[:], ALU.add))
                for i, (dst, a, b_, op) in enumerate(tensors):
                    wait(pool, s_stat, STATS * b + i)
                    nc.gpsimd.tensor_tensor(dst, a, b_, op).then_inc(s_stat, 1)
                wait(pool, s_stat, STATS * b + len(tensors))
                pool.sem_inc(s_go_var, 1)
                nc.gpsimd.tensor_scalar(var[c % 2][:], pool_c[:], 0.0, None, ALU.max).then_inc(s_stat, 1)

            def lower_parts(b, c, k):
                wait(pool, s_upper, H * b + k + 1)
                wait(pool, s_tabT_ps, TFILLS * (b - 1))
                g = slice(GH * k, GH * (k + 1))
                nc.gpsimd.tensor_tensor(parts[c % 2][:, g, 1, :], table[c % 2][:, g, :], parts[c % 2][:, g, 0, :],
                                        ALU.subtract).then_inc(s_lower, 1)

            def scaled_sum(b, c):
                wait(pool, s_z, b + 1)
                wait(pool, s_y, 3 * b)
                scale = scaler[:, bass.ds(H * b, H), :].unsqueeze(3).to_broadcast([P, H, 2, D])
                nc.gpsimd.tensor_tensor(zs[:], z[c % 2][:, :, 1:3, :], scale, ALU.mult).then_inc(s_y, 1)
                wait(pool, s_y, 3 * b + 1)
                nc.gpsimd.tensor_tensor(y1[:], z[c % 2][:, :, 0, :], zs[:, :, 0, :], ALU.add).then_inc(s_y, 1)
                wait(pool, s_y, 3 * b + 2)
                wait(pool, s_res, b - 1)
                nc.gpsimd.tensor_tensor(y[c % 2][:], y1[:], zs[:, :, 1, :], ALU.add).then_inc(s_y, 1)

            def normalise(b, c):
                wait(pool, s_rstd, b + 1)
                wait(pool, s_out[c % 2], half(b, c) - 16)
                nc.gpsimd.tensor_tensor(result[c % 2][:], y[c % 2][:], rstd[:, c % 2, :].unsqueeze(2).to_broadcast([P, H, D]),
                                        ALU.mult).then_inc(s_res, 1)

            def degree_tree(c):
                pool.wait_ge(s_all[c % 2], 16 * (c // 2 + 1))
                rows = adj_all[:, c % 2].rearrange("p b t m -> p (b t) m")
                for i in range(TREE):
                    wait(pool, s_tree, TREE * (c - DVE_CHUNKS) + i)
                    k = N >> i + 1
                    to = rows[:, :, 0:k] if k > 1 else deg[:, H * CH * c:H * CH * (c + 1)].unsqueeze(2)
                    nc.gpsimd.tensor_tensor(to, rows[:, :, 0:k], rows[:, :, k:2 * k], ALU.add).then_inc(s_tree, 1)

            def one_step(s, c, has):
                if at(s, 1):
                    neighbours(s, c)
                if "Q" in has:
                    lower_parts(s - 1, c - 1, 1)
                    if at(s, 1):
                        pool.wait_ge(s_deg, DEG_FIRST)
                    if at(s, 5):
                        pool.wait_ge(s_deg, DEG_SECOND)
                    if at(s, 7):
                        pool.wait_ge(s_deg, DEG_ALL)
                    statistics(s - 1, c - 1)
                if "P" in has and not at(s, 1):
                    neighbours(s, c)
                if "Z" in has:
                    if at(s, 3):
                        pool.wait_ge(s_log, 3)
                    scaled_sum(s - 3, c - 3)
                if isinstance(s, int) and TREE_FIRST <= s < TREE_FIRST + CHUNKS - DVE_CHUNKS:
                    degree_tree(DVE_CHUNKS + s - TREE_FIRST)
                if "Z" in has:
                    normalise(s - 3, c - 3)
                if "P" in has:
                    lower_parts(s, c, 0)
                if at(s, 7):
                    pool.wait_ge(s_log, 6)

            steps(pool, one_step)


_INS = ["x", "adj", "L0_gnn_W_pre", "L0_gnn_b_pre", "L0_gnn_W_post", "L0_gnn_b_post"]


def kernel(**inputs):
    import numpy as _np
    import concourse.bacc as _bacc
    from concourse import mybir as _mybir
    from concourse.bass_utils import run_bass_kernel_spmd as _run

    nc = _bacc.Bacc("TRN2", target_bir_lowering=False, num_devices=1)
    arrays, args = {}, []
    given = [(name, inputs[name]) for name in _INS] + list(zip(("ident", "sign", "bias"), constants()))
    for name, a in given:
        a = _np.ascontiguousarray(a)
        arrays[f"in_{name}_dram"] = a
        args.append(nc.dram_tensor(f"in_{name}_dram", a.shape, _mybir.dt.from_np(a.dtype), kind="ExternalInput").ap())
    args.append(nc.dram_tensor("out_0_dram", (B, N, D), F32, kind="ExternalOutput").ap())
    pna_layer(nc, *args)
    r = _run(nc, [arrays], core_ids=[0])
    return r.results[0]["out_0_dram"]
```
